# Optimizing a Trainium2 kernel written in Bass

```python
import numpy as np
import jax
import jax.numpy as jnp

def _softmax(x, axis=-1):
    return jax.nn.softmax(x, axis=axis)

def _gelu(x):
    return jax.nn.gelu(x, approximate=True)

def _silu(x):
    return jax.nn.silu(x)

def _sigmoid(x):
    return jax.nn.sigmoid(x)

def _layernorm(x, axis=-1, eps=1e-05):
    m = jnp.mean(x, axis=axis, keepdims=True)
    v = jnp.var(x, axis=axis, keepdims=True)
    return (x - m) / jnp.sqrt(v + eps)

def _scatter_add(tgt, idx, src, axis=0):
    return tgt.at[idx].add(src)

def _segment_sum(src, seg, n):
    return jax.ops.segment_sum(src, seg, n)
kernel_name = 'mk_flamingo_gated_d1_seqx_r8_f5b7fb'

def setup_inputs(seed: int=0):
    np.random.seed(seed)
    _w = jnp.asarray

    def _rec_inputs():
        import jax
        import jax.numpy as jnp
        _rk = jax.random.key(seed)
        x = -0.0002928 + 1 * jax.random.normal(jax.random.fold_in(_rk, 1), (32, 64, 256), jnp.float32)
        _lenS = 64 - jax.random.randint(jax.random.fold_in(_rk, 7), (32,), 0, max(1, 64 // 4) + 1, jnp.int32)
        _lenS2 = 64 - jax.random.randint(jax.random.fold_in(_rk, 8), (32,), 0, max(1, 64 // 4) + 1, jnp.int32)
        _ctx_2048P = jax.random.normal(jax.random.fold_in(_rk, 11), (32, 16, 256), jnp.float32)
        _ctx_2048c = jax.random.dirichlet(jax.random.fold_in(_rk, 511), 0.3 * jnp.ones((16,), jnp.float32), (32, 64))
        _ctx_2048t = jnp.einsum('bsk,bkd->bsd', _ctx_2048c, _ctx_2048P)
        _ctx_2048t = _ctx_2048t * jax.lax.rsqrt(jnp.mean(jnp.square(_ctx_2048t)) + 1e-12) * 0.953939
        ctx_2048 = -1.39393e-06 + 0.999914 * (_ctx_2048t + 0.3 * jax.random.normal(jax.random.fold_in(_rk, 611), (32, 64, 256), jnp.float32))
        _g = jax.random.normal(jax.random.fold_in(_rk, 9001), (2, 1), jnp.float32)
        _g = jnp.sign(_g) * jnp.maximum(jnp.abs(_g), 1.0) + (_g == 0) * 1.0
        g_xattn = _g[0]
        g_ffn = _g[1]
        return (x, ctx_2048, g_xattn, g_ffn)
    x, ctx_2048, g_xattn, g_ffn = _rec_inputs()

    def _L0_xattn_setup():
        import math
        import jax, jax.numpy as jnp
        import numpy as np
        N_HEADS = 8
        CHANNELS = 64
        K_CH = CHANNELS // N_HEADS
        THETA = 10000.0

        def _rope_freqs(length, dim):
            inv_freq = 1.0 / THETA ** (jnp.arange(0, dim, 2, dtype=jnp.float32) / dim)
            f = jnp.arange(length, dtype=jnp.float32)[:, None] * inv_freq[None, :]
            return jnp.concatenate([f, f], axis=-1)

        def _apply_rotary(pos, t):
            half = t.shape[-1] // 2
            rot = jnp.concatenate([-t[..., half:], t[..., :half]], axis=-1)
            return t * jnp.cos(pos) + rot * jnp.sin(pos)

        def _proj(inp, W, b):
            return jnp.einsum('oc,bct->bot', W, inp) + b[None, :, None]
        key = jax.random.key(seed)
        ks = jax.random.split(key, 10)
        B, C, T = (4, CHANNELS, 256)
        bound = math.sqrt(6.0 / (C + C))

        def w(k):
            return jax.random.uniform(k, (C, C), jnp.float32, -bound, bound)
        return {'x': jax.random.normal(ks[0], (B, C, T), jnp.float32), 'c': jax.random.normal(ks[1], (B, C, T), jnp.float32), 'Wq': w(ks[2]), 'bq': jnp.zeros((C,), jnp.float32), 'Wk': w(ks[3]), 'bk': jnp.zeros((C,), jnp.float32), 'Wv': w(ks[4]), 'bv': jnp.zeros((C,), jnp.float32), 'Wo': w(ks[5]), 'bo': jnp.zeros((C,), jnp.float32)}
    _L0_xattn_all = _L0_xattn_setup()
    _L0_xattn_in = {k: v for k, v in _L0_xattn_all.items() if k in ('Wq', 'bq', 'Wk', 'bk', 'Wv', 'bv', 'Wo', 'bo')}
    del _L0_xattn_all

    def _L0_ffn_setup():
        import jax, jax.numpy as jnp
        import numpy as np
        TOP_K = 2
        key = jax.random.key(seed)
        ks = jax.random.split(key, 5)
        B, T, D, E, H = (4, 256, 256, 8, 176)
        s = 1.0 / np.sqrt(D)
        sh = 1.0 / np.sqrt(H)
        return {'x': jax.random.normal(ks[0], (B, T, D), dtype=jnp.float32), 'Wg': jax.random.normal(ks[1], (E, D), dtype=jnp.float32) * s, 'W1': jax.random.normal(ks[2], (E, H, D), dtype=jnp.float32) * s, 'W2': jax.random.normal(ks[3], (E, H, D), dtype=jnp.float32) * s, 'W3': jax.random.normal(ks[4], (E, D, H), dtype=jnp.float32) * sh}
    _L0_ffn_all = _L0_ffn_setup()
    _L0_ffn_in = {k: v for k, v in _L0_ffn_all.items() if k in ('Wg', 'W1', 'W2', 'W3')}
    del _L0_ffn_all
    return {'x': x, 'ctx_2048': ctx_2048, 'g_xattn': g_xattn, 'g_ffn': g_ffn, 'L0_xattn_Wq': _L0_xattn_in['Wq'], 'L0_xattn_bq': _L0_xattn_in['bq'], 'L0_xattn_Wk': _L0_xattn_in['Wk'], 'L0_xattn_bk': _L0_xattn_in['bk'], 'L0_xattn_Wv': _L0_xattn_in['Wv'], 'L0_xattn_bv': _L0_xattn_in['bv'], 'L0_xattn_Wo': _L0_xattn_in['Wo'], 'L0_xattn_bo': _L0_xattn_in['bo'], 'L0_ffn_Wg': _L0_ffn_in['Wg'], 'L0_ffn_W1': _L0_ffn_in['W1'], 'L0_ffn_W2': _L0_ffn_in['W2'], 'L0_ffn_W3': _L0_ffn_in['W3']}

def reference(x, ctx_2048, g_xattn, g_ffn, L0_xattn_Wq, L0_xattn_bq, L0_xattn_Wk, L0_xattn_bk, L0_xattn_Wv, L0_xattn_bv, L0_xattn_Wo, L0_xattn_bo, L0_ffn_Wg, L0_ffn_W1, L0_ffn_W2, L0_ffn_W3):
    import jax
    import jax.numpy as jnp

    def _L0_xattn_ref(x, c, Wq, bq, Wk, bk, Wv, bv, Wo, bo):
        import math
        import jax, jax.numpy as jnp
        import numpy as np
        N_HEADS = 8
        CHANNELS = 64
        K_CH = CHANNELS // N_HEADS
        THETA = 10000.0

        def _rope_freqs(length, dim):
            inv_freq = 1.0 / THETA ** (jnp.arange(0, dim, 2, dtype=jnp.float32) / dim)
            f = jnp.arange(length, dtype=jnp.float32)[:, None] * inv_freq[None, :]
            return jnp.concatenate([f, f], axis=-1)

        def _apply_rotary(pos, t):
            half = t.shape[-1] // 2
            rot = jnp.concatenate([-t[..., half:], t[..., :half]], axis=-1)
            return t * jnp.cos(pos) + rot * jnp.sin(pos)

        def _proj(inp, W, b):
            return jnp.einsum('oc,bct->bot', W, inp) + b[None, :, None]
        b, _, t_t = x.shape
        t_s = c.shape[2]
        q_emb = _rope_freqs(t_t, K_CH)
        k_emb = _rope_freqs(t_s, K_CH)

        def split_heads(t):
            return t.reshape(b, N_HEADS, K_CH, t.shape[2]).transpose(0, 1, 3, 2)
        q = split_heads(_proj(x, Wq, bq))
        k = split_heads(_proj(c, Wk, bk))
        v = split_heads(_proj(c, Wv, bv))
        q = _apply_rotary(q_emb, q)
        k = _apply_rotary(k_emb, k)
        scores = jnp.einsum('bhtc,bhsc->bhts', q, k) / math.sqrt(K_CH)
        p_attn = jax.nn.softmax(scores, axis=-1)
        out = jnp.einsum('bhts,bhsc->bhtc', p_attn, v)
        out = out.transpose(0, 1, 3, 2).reshape(b, N_HEADS * K_CH, t_t)
        return _proj(out, Wo, bo)

    def _L0_ffn_ref(x, Wg, W1, W2, W3):
        import jax, jax.numpy as jnp
        import numpy as np
        TOP_K = 2
        E = Wg.shape[0]
        scores = jnp.einsum('btd,ed->bte', x, Wg)
        topk_s, topk_i = jax.lax.top_k(scores, TOP_K)
        probs = jax.nn.softmax(topk_s, axis=-1)
        onehot = (topk_i[..., None] == jnp.arange(E)).astype(x.dtype)
        w = jnp.einsum('btk,btke->bte', probs, onehot)
        y = jnp.zeros_like(x)
        for e in range(E):
            h = jax.nn.silu(jnp.einsum('btd,hd->bth', x, W1[e])) * jnp.einsum('btd,hd->bth', x, W2[e])
            y = y + w[..., e:e + 1] * jnp.einsum('bth,dh->btd', h, W3[e])
        return y
    x = x + jnp.tanh(g_xattn[0]) * _L0_xattn_ref(_layernorm(x, axis=-1), ctx_2048, L0_xattn_Wq, L0_xattn_bq, L0_xattn_Wk, L0_xattn_bk, L0_xattn_Wv, L0_xattn_bv, L0_xattn_Wo, L0_xattn_bo)
    x = x + jnp.tanh(g_ffn[0]) * _L0_ffn_ref(_layernorm(x, axis=-1), L0_ffn_Wg, L0_ffn_W1, L0_ffn_W2, L0_ffn_W3)
    return x

_drawn_inputs = setup_inputs


def setup_inputs(seed=0):
    import zlib

    import numpy as np

    out = dict(_drawn_inputs(seed))
    spreads = {'L0_xattn_bq': (0.0, 0.1),
     'L0_xattn_bk': (0.0, 0.1),
     'L0_xattn_bv': (0.0, 0.1),
     'L0_xattn_bo': (0.0, 0.1)}
    factors = {}
    for name, (base, spread) in spreads.items():
        noise = np.random.default_rng([zlib.crc32(name.encode()), seed]).standard_normal(out[name].shape)
        drawn = base * np.exp(spread * noise) if base else spread * noise
        out[name] = jnp.asarray(drawn.astype(out[name].dtype))
    for name, factor in factors.items():
        out[name] = (out[name] * factor).astype(out[name].dtype)
    return out
```

```python
from contextlib import ExitStack

import numpy as np

import concourse.bass as bass
from concourse import mybir

F32 = mybir.dt.float32
F32R = mybir.dt.float32r
BF16 = mybir.dt.bfloat16
U32 = mybir.dt.uint32
ALU = mybir.AluOpType
ACT = mybir.ActivationFunctionType
AX = mybir.AxisListType

B, C, T = 32, 64, 256
HEADS, KCH = 8, 8
E, HID = 8, 176
P = 128
PAIRS = B // 2
GH = 4
GPP = 2 * HEADS // GH
GROUPS = PAIRS * GPP
TC = T // P
SCALE = float(KCH) ** -0.5
EPS = 1e-5
FCH = E * HID // P
UP = 2 * HID
ROUTES = 9
MROW = 3 * KCH

C_COS, C_SIN, C_SEL, C_ID, C_ONE, C_IOTA = 0, T, 2 * T, 2 * T + 16 * P, 2 * T + 17 * P, 2 * T + 17 * P + 1
C_ALL = C_IOTA + E


def constants():
    inv = np.float32(1.0) / np.power(np.float32(10000.0), np.arange(0, KCH, 2, dtype=np.float32) / np.float32(KCH))
    f = np.arange(T, dtype=np.float32)[:, None] * inv.astype(np.float32)[None, :]
    f = np.concatenate([f, f], axis=-1)
    sign = np.where(np.arange(KCH) < KCH // 2, -1.0, 1.0).astype(np.float32)
    out = np.zeros((P, C_ALL), np.float32)
    out[:, C_COS:C_COS + T] = np.tile(np.cos(f).T, (P // KCH, 1))
    out[:, C_SIN:C_SIN + T] = np.tile((np.sin(f) * sign).T, (P // KCH, 1))
    rows = ((0, 1), (2,), (0, 2), (1,))
    sel = np.zeros((P, 4, GPP, P), np.float32)
    for kind in range(4):
        for g in range(GPP):
            for j in range(GH):
                for r in rows[kind]:
                    for c in range(KCH):
                        sel[g * GH * KCH + j * KCH + c, kind, g, 32 * j + r * KCH + c] = 1.0
    out[:, C_SEL:C_SEL + 16 * P] = sel.reshape(P, 16 * P)
    out[:, C_ID:C_ID + P] = np.eye(P, dtype=np.float32)
    for j in range(GH):
        out[32 * j + MROW:32 * j + MROW + 2, C_ONE] = 1.0
    out[:, C_IOTA:C_IOTA + E] = np.arange(E, dtype=np.float32)
    return out


class Pair:

    def __init__(self, v, least=None):
        self.v, self.least, self.known = v, least, least is None

    def __add__(self, n):
        return Pair(self.v + n, None if self.known else self.least + n)

    def __sub__(self, n):
        return Pair(self.v - n, None if self.known else self.least - n)

    def times(self, per, plus):
        assert (per * self.v if self.known else per * self.least) + plus > 0
        return self.v * per + plus if plus else self.v * per

    def after(self, per, plus):
        if self.known:
            return per * self.v + plus > 0
        assert per * self.least + plus > 0
        return True


def build(nc, x, ctx_in, w_proj, w_o, vecs, bv, gates, w_up, w_down, const, out):
    x_d = x.rearrange("(n b) c t -> n (b c) t", b=2)
    c_d = ctx_in.rearrange("(n b) c t -> n (b c) t", b=2)
    o_d = out.rearrange("(n b) c t -> n (b c) t", b=2)

    with ExitStack() as stack:
        def sb(name, shape, dt=F32):
            return stack.enter_context(nc.sbuf_tensor(name, shape, dt))

        def bank(name):
            return stack.enter_context(nc.psum_tensor(name, [P, 512], F32))

        def sem(name):
            return stack.enter_context(nc.semaphore(name))

        cst = sb("cst", [P, C_ALL])
        cosT, sinT = cst[:, C_COS:C_COS + T], cst[:, C_SIN:C_SIN + T]
        ident = cst[:, C_ID:C_ID + P]
        m_rows_one = cst[:, C_ONE:C_ONE + 1]
        iota8 = cst[:, C_IOTA:C_IOTA + E]
        sel_r = sb("sel_r", [P, 4, GPP, P], F32R)
        ident_b = sb("ident_b", [P, P], BF16)
        wp = sb("wp", [P, 5, P])
        wo = sb("wo", [P, 2, C])
        vec = sb("vec", [P, 5])
        bvb = sb("bvb", [P, TC, 2 * HEADS, KCH])
        gts = sb("gts", [P, 2])
        tg = sb("tg", [P, 2])
        tgo = sb("tgo", [P, 1])
        tgh = sb("tgh", [P, 1])
        wup = sb("wup", [P, 2, E + E * UP])
        wdn = sb("wdn", [P, FCH, T])
        xt = sb("xt", [P, 2, T])
        ct = sb("ct", [P, 2, T])
        stats = sb("stats", [P, 6])
        mv = sb("mv", [P, 2])
        rstd = sb("rstd", [P, 1])
        xn = sb("xn", [P, T])
        rot_a = sb("rot_a", [P, 2, T])
        rot_b = sb("rot_b", [P, 2, T])
        roped = sb("roped", [P, 2, T])
        qk_hi = sb("qk_hi", [P, 2, 2, T], F32R)
        qk_lo = sb("qk_lo", [P, 2, 2, T], F32R)
        vE = sb("vE", [P, 2, TC, 2 * HEADS, 32])
        xres = sb("xres", [P, 2, T])
        qS = sb("qS", [P, 2, T], F32R)
        qM = sb("qM", [P, 2, T], F32R)
        kM = sb("kM", [P, 2, GH, T], F32R)
        negm = sb("negm", [P, GH, TC])
        mpl = sb("mpl", [P, TC, P], BF16)
        probs = sb("probs", [P, 2, GH, TC, T])
        powers = sb("powers", [P, 2])
        veps, veps2 = sb("veps", [P, 1]), sb("veps2", [P, 1])
        oT = sb("oT", [P, T])
        rden = sb("rden", [P, T // 32, 1])
        att = sb("att", [P, GPP, T])
        x1 = sb("x1", [P, 2, T])
        stats2 = sb("stats2", [P, 6])
        mv2 = sb("mv2", [P, 2])
        rstd2 = sb("rstd2", [P, 1])
        xn2 = sb("xn2", [P, T])
        xT2 = sb("xT2", [P, 2, P])
        sc8 = sb("sc8", [P, E])
        top8 = sb("top8", [P, 8])
        idx8 = sb("idx8", [P, 8], U32)
        idxf = sb("idxf", [P, 2])
        rt = sb("rt", [P, 8])
        oh = sb("oh", [P, 2, E])
        wts = sb("wts", [P, E])
        th = sb("th", [P, 2, HID])
        ug = sb("ug", [P, 2, HID])
        hid = sb("hid", [P, E * HID])
        hT = sb("hT", [P, FCH, P])

        s_bank = [bank("s_bank0"), bank("s_bank1")]
        st_bank = [bank("st_bank0"), bank("st_bank1")]
        pv_bank = bank("pv_bank")
        up_bank = [bank("up_bank0"), bank("up_bank1")]
        misc = bank("misc")

        w_in = sem("w_in")
        x_in = [sem("x_in0"), sem("x_in1")]
        stored = [sem("stored0"), sem("stored1")]
        zeroed = sem("zeroed")
        waits_over = sem("waits_over")
        tanh_g = sem("tanh_g")
        gates_ready = sem("gates_ready")
        consts_r = sem("consts_r")
        q_proj, k_proj, v_proj = sem("q_proj"), sem("k_proj"), sem("v_proj")
        stacked, scored, scoredT = sem("stacked"), sem("scored"), sem("scoredT")
        m_turned, pv_done, o_done = sem("m_turned"), sem("pv_done"), sem("o_done")
        x2_turned, up_done, h_turned, y_done = sem("x2_turned"), sem("up_done"), sem("h_turned"), sem("y_done")
        stack_copied, exp_done = sem("stack_copied"), sem("exp_done")
        x2_copied, sc_copied, tanh_done = sem("x2_copied"), sem("sc_copied"), sem("tanh_done")
        h_copied, dexp_done = sem("h_copied"), sem("dexp_done")
        ln1, ln2 = sem("ln1"), sem("ln2")
        q_roped, k_roped, v_copied = sem("q_roped"), sem("k_roped"), sem("v_copied")
        reduced, m_split, m_added = sem("reduced"), sem("m_split"), sem("m_added")
        turned_out, inverted, divided, normed, x1_done = sem("turned_out"), sem("inverted"), sem("divided"), sem("normed"), sem("x1_done")
        top2, u_done, h_done, y_added = sem("top2"), sem("u_done"), sem("h_done"), sem("y_added")
        root1, root2, pool_consts = sem("root1"), sem("root2"), sem("pool_consts")
        q_split, k_split, xres_done, routed = sem("q_split"), sem("k_split"), sem("xres_done"), sem("routed")

        W_DMAS = 2 + HEADS + 6

        LOOP_FROM = 2
        LOOP_TO = PAIRS - 2

        def settled(eng):
            eng.sem_inc(waits_over, 1)

        def bodies(eng, body):
            body(Pair(0), 0)
            body(Pair(1), 1)
            with eng.Fori(LOOP_FROM // 2, LOOP_TO // 2) as i:
                body(Pair(i * 2, LOOP_FROM), 0)
                body(Pair(i * 2 + 1, LOOP_FROM + 1), 1)
            for p in range(LOOP_TO, PAIRS + 2):
                body(Pair(p), p % 2)

        def at(p, low, high):
            if p.known:
                return low <= p.v <= high
            assert low <= LOOP_FROM and high >= LOOP_TO - 1
            return True

        def scores_here(p):
            return at(p, 0, PAIRS - 1)

        def before_here(p, g):
            return at(p, 0 if g else 1, PAIRS if g == 0 else PAIRS - 1)

        def norm_here(p, g):
            return at(p, 0 if g > 1 else 1, PAIRS if g < 2 else PAIRS - 1)

        def next_here(p):
            return at(p, 0, PAIRS - 2)

        def prev_here(p):
            return at(p, 1, PAIRS)

        def prev2_here(p):
            return at(p, 2, PAIRS + 1)

        block = stack.enter_context(nc.Block())

        @block.sync
        def _(sp):
            def load(p, par):
                if p.after(1, -1):
                    sp.wait_ge(xres_done, p.times(1, -1))
                    settled(sp)
                if p.after(3, -3):
                    sp.wait_ge(ln1, p.times(3, -3))
                    settled(sp)
                if p.after(1, -1):
                    sp.wait_ge(v_proj, p.times(1, -1))
                    settled(sp)
                sp.dma_start(xt[:, par, :], x_d[p.v, :, :]).then_inc(x_in[par], 16)
                sp.dma_start(ct[:, par, :], c_d[p.v, :, :]).then_inc(x_in[par], 16)

            load(Pair(0), 0)
            sp.wait_ge(zeroed, 1)
            for b in range(2):
                sp.dma_start(wp[b * C:(b + 1) * C, :, b * C:(b + 1) * C],
                             w_proj.rearrange("c (n o) -> c n o", n=5)).then_inc(w_in, 16)
            sp.dma_start(vec[:], vecs).then_inc(w_in, 16)
            sp.dma_start(cst[:], const).then_inc(w_in, 16)
            load(Pair(1), 1)
            sp.dma_start(gts[:], gates.to_broadcast([P, 2])).then_inc(w_in, 16)
            sp.dma_start(bvb[:].rearrange("p s h c -> p (s h c)"), bv.to_broadcast([P, TC * 2 * C])).then_inc(w_in, 16)
            for h in range(HEADS):
                g, j = divmod(h, GH)
                sp.dma_start(wo[32 * j:32 * j + KCH, g, :], w_o[h * KCH:(h + 1) * KCH, :]).then_inc(w_in, 16)
            sp.dma_start(wup[:], w_up.rearrange("(k p) n -> p k n", p=P)).then_inc(w_in, 16)
            sp.dma_start(wdn[:], w_down.rearrange("(k p) n -> p k n", p=P)).then_inc(w_in, 16)

            def body(p, par):
                if prev2_here(p):
                    sp.wait_ge(y_added, p.times(1, -1))
                    settled(sp)
                    sp.dma_start(o_d[(p - 2).v, :, :], x1[:, par, :]).then_inc(stored[par], 16)
                if at(p, 0, PAIRS - 3):
                    if prev2_here(p):
                        sp.wait_ge(stored[par], (p - 2).times(8, 16 - 8 * (par)))
                        settled(sp)
                    load(p + 2, par)

            bodies(sp, body)
            sp.wait_ge(stored[0], 16 * (PAIRS // 2))
            sp.wait_ge(stored[1], 16 * (PAIRS // 2))

        @block.tensor
        def _(pe):
            def score(p, g, h):
                G4 = 4 * g + h
                par = g % 2
                if h == 0:
                    pe.wait_ge(stack_copied, p.times(4, g + 1))
                if p.after(16, G4 - 1):
                    pe.wait_ge(reduced, p.times(16, G4 - 1))
                for t in range(TC):
                    mm = pe.matmul(s_bank[h % 2][:, t * T:(t + 1) * T], qS[:, par, t * P:(t + 1) * P],
                                   kM[:, par, h, :], start=True, stop=True)
                mm.then_inc(scored, 1)

            def score_t(p, g, h):
                n = 4 * (g - 1) + h
                par = (g - 1) % 2
                if h == 0:
                    pe.wait_ge(m_added, p.times(4, g))
                if p.after(16, n - 1):
                    pe.wait_ge(exp_done, p.times(16, n - 1))
                for s in range(TC):
                    mm = pe.matmul(st_bank[h % 2][:, s * T:(s + 1) * T], kM[:, par, h, s * P:(s + 1) * P],
                                   qM[:, par, :], start=True, stop=True)
                mm.then_inc(scoredT, 1)

            def weigh(p, g):
                par = (g - 1) % 2
                vpar = PARITY[0] if g else 1 - PARITY[0]
                gg = (g - 1) % GPP
                pe.wait_ge(exp_done, p.times(16, 4 * g))
                if p.after(4, g - 1):
                    pe.wait_ge(turned_out, p.times(4, g - 1))
                for s in range(TC):
                    for j in range(GH):
                        mm = pe.matmul(pv_bank[32 * j:32 * j + 32, (gg % 2) * T:(gg % 2) * T + T],
                                       vE[:, vpar, s, gg * GH + j, :], probs[:, par, j, s, :],
                                       start=(s == 0), stop=(s == TC - 1))
                mm.then_inc(pv_done, 1)

            def turn_m(p, g):
                pe.wait_ge(m_split, p.times(8, 2 * g + 2))
                if p.after(16, 4 * g - 1):
                    pe.wait_ge(exp_done, p.times(16, 4 * g - 1))
                for t in range(TC):
                    mm = pe.matmul(st_bank[0][:, t * P:(t + 1) * P], mpl[:, t, :], ident_b[:],
                                   start=True, stop=True)
                mm.then_inc(m_turned, 1)

            def stack_qk(p, g, par):
                if g == 0:
                    pe.wait_ge(q_split, p.times(3, 3))
                    pe.wait_ge(k_split, p.times(3, 3))
                for n in range(2):
                    for part, src in enumerate((qk_hi, qk_lo)):
                        mm = pe.matmul(misc[:, n * T:(n + 1) * T], sel_r[:, 2 * n + part, g, :], src[:, par, n, :],
                                       start=(part == 0), stop=(part == 1))
                mm.then_inc(stacked, 1)

            def project(p, par, n):
                src = xn[:] if n == 0 else ct[:, par, :]
                if n == 0:
                    pe.wait_ge(ln1, p.times(3, 3))
                else:
                    pe.wait_ge(x_in[par], p.times(16, 32 - 16 * par))
                for r in range(2):
                    mm = pe.matmul(misc[:, r * T:(r + 1) * T], wp[:, 2 * n + r, :], src, start=True, stop=True)
                mm.then_inc(q_proj if n == 0 else k_proj, 1)

            def project_v(p, par):
                for s in range(TC):
                    mm = pe.matmul(misc[:, s * P:(s + 1) * P], ct[:, par, s * P:(s + 1) * P], wp[:, 4, :],
                                   start=True, stop=True)
                mm.then_inc(v_proj, 1)

            def project_o(p):
                pe.wait_ge(normed, p.times(4, 4))
                if p.after(8, -1):
                    pe.wait_ge(h_done, p.times(8, -1))
                for g in range(2):
                    for b in range(2):
                        mm = pe.matmul(up_bank[0][b * C:(b + 1) * C, 0:T], wo[:, g, :], att[:, 2 * b + g, :],
                                       start=(g == 0), stop=(g == 1))
                mm.then_inc(o_done, 1)

            def turn_x2(p):
                pe.wait_ge(ln2, p.times(3, 3))
                if p.after(1, 0):
                    pe.wait_ge(y_added, p.times(1, 0))
                for k in range(2):
                    mm = pe.transpose(up_bank[1][:, k * P:(k + 1) * P], xn2[:, k * P:(k + 1) * P], ident)
                mm.then_inc(x2_turned, 1)

            def up(p, e):
                if e == 0:
                    pe.wait_ge(x2_copied, p.times(1, 1))
                if p.after(8, e - 1):
                    pe.wait_ge(h_done, p.times(8, e - 1))
                cols = (0, E + UP) if e == 0 else (E + e * UP, E + (e + 1) * UP)
                at_ = 0 if e == 0 else E
                for k in range(2):
                    mm = pe.matmul(up_bank[e % 2][:, at_:E + UP], xT2[:, k, :], wup[:, k, cols[0]:cols[1]],
                                   start=(k == 0), stop=(k == 1))
                mm.then_inc(up_done, 1)

            def turn_h(p, r):
                if r == 0:
                    pe.wait_ge(h_done, p.times(8, 8))
                else:
                    pe.wait_ge(h_copied, p.times(3, r))
                for k in range(4 * r, min(4 * r + 4, FCH)):
                    mm = pe.transpose(up_bank[1][:, (k % 4) * P:(k % 4 + 1) * P], hid[:, k * P:(k + 1) * P], ident)
                mm.then_inc(h_turned, 1)

            def down(p):
                pe.wait_ge(h_copied, p.times(3, 3))
                for k in range(FCH):
                    mm = pe.matmul(up_bank[1][:, 0:T], hT[:, k, :], wdn[:, k, :], start=(k == 0), stop=(k == FCH - 1))
                mm.then_inc(y_done, 1)

            PARITY = [0]

            def body(p, par):
                PARITY[0] = par
                for g in range(GPP):
                    for h in range(GH):
                        if scores_here(p):
                            score(p, g, h)
                        if before_here(p, g):
                            score_t(p, g, h)
                        if next_here(p) and h == 0 and g:
                            pe.wait_ge(stack_copied, p.times(4, g + 1))
                            if g < 3:
                                project(p + 1, 1 - par, g - 1)
                            else:
                                project_v(p + 1, 1 - par)
                        if prev2_here(p):
                            if g == 0 and h < 3:
                                up(p - 2, 5 + h)
                            if g == 1 and h < 3:
                                turn_h(p - 2, h)
                            if g == 1 and h == 3:
                                down(p - 2)
                        if prev_here(p):
                            if g == 1 and h == 2:
                                project_o(p - 1)
                            if g == 2 and h == 1:
                                turn_x2(p - 1)
                            if g == 2 and h > 1:
                                up(p - 1, h - 2)
                            if g == 3 and h > 0:
                                up(p - 1, 1 + h)
                    if scores_here(p):
                        if g == 0:
                            pe.wait_ge(stack_copied, p.times(4, 1))
                            stack_qk(p, 1, par)
                        elif g < 3:
                            if not next_here(p):
                                pe.wait_ge(stack_copied, p.times(4, g + 1))
                            elif g == 1:
                                pe.wait_ge(q_roped, p.times(1, 2))
                            else:
                                pe.wait_ge(k_roped, p.times(1, 2))
                            stack_qk(p, g + 1, par)
                        elif next_here(p):
                            pe.wait_ge(v_copied, p.times(1, 2))
                            stack_qk(p + 1, 0, 1 - par)
                        turn_m(p, g)
                    if before_here(p, g):
                        weigh(p, g)

            pe.wait_ge(w_in, 16 * W_DMAS)
            pe.wait_ge(zeroed, 1)
            project(Pair(0), 0, 0)
            pe.wait_ge(q_roped, 1)
            project(Pair(0), 0, 1)
            pe.wait_ge(k_roped, 1)
            project_v(0, 0)
            pe.wait_ge(v_copied, 1)
            pe.wait_ge(consts_r, 1)
            stack_qk(Pair(0), 0, 0)
            bodies(pe, body)

        @block.scalar
        def _(act):
            def expo(p, g, h):
                n = 4 * (g - 1) + h
                act.wait_ge(scoredT, p.times(16, n + 1))
                if p.after(4, g - 2):
                    act.wait_ge(pv_done, p.times(4, g - 2))
                nc.scalar.activation(probs[:, (g - 1) % 2, h, :, :].rearrange("p s t -> p (s t)"), st_bank[h % 2][:],
                                     ACT.Exp, scale=SCALE).then_inc(exp_done, 1)

            def copy_stack(p, g):
                par = g % 2
                act.wait_ge(stacked, p.times(4, g + 1))
                if p.after(16, 4 * (g - 1)):
                    act.wait_ge(scoredT, p.times(16, 4 * (g - 1)))
                if p.after(4, g - 1):
                    act.wait_ge(m_added, p.times(4, g - 1))
                nc.scalar.activation(qS[:, par, :], misc[:, 0:T], ACT.Identity)
                for j in range(GH):
                    rows = slice(32 * j, 32 * j + 32)
                    last = nc.scalar.activation(kM[rows, par, j, :], misc[rows, T:2 * T], ACT.Identity,
                                                bias=m_rows_one[rows, :])
                last.then_inc(stack_copied, 1)

            def tanh(p, e):
                act.wait_ge(up_done, p.times(8, e + 1))
                if p.after(8, e - 1):
                    act.wait_ge(u_done, p.times(8, e - 1))
                nc.scalar.activation(th[:, e % 2, :], up_bank[e % 2][:, E:E + HID], ACT.Tanh,
                                     scale=0.5).then_inc(tanh_done, 1)

            def body(p, par):
                for g in range(GPP):
                    for h in range(GH):
                        if before_here(p, g):
                            expo(p, g, h)
                        if prev2_here(p):
                            if g == 0 and h < 3:
                                tanh(p - 2, 5 + h)
                            if g == 1 and h < 3:
                                act.wait_ge(h_turned, (p - 2).times(3, h + 1))
                                n = min(4, FCH - 4 * h) * P
                                nc.scalar.activation(hT[:, 4 * h:4 * h + n // P, :].rearrange("p k t -> p (k t)"),
                                                     up_bank[1][:, 0:n], ACT.Identity).then_inc(h_copied, 1)
                        if prev_here(p):
                            if g == 2 and h == 1:
                                act.wait_ge(x2_turned, p.times(1, 0))
                                if p.after(8, -8):
                                    act.wait_ge(up_done, p.times(8, -8))
                                nc.scalar.activation(xT2[:].rearrange("p k t -> p (k t)"), up_bank[1][:, 0:2 * P],
                                                     ACT.Identity).then_inc(x2_copied, 1)
                            if g == 2 and h == 2:
                                act.wait_ge(up_done, p.times(8, -7))
                                if p.after(2, -2):
                                    act.wait_ge(top2, p.times(2, -2))
                                nc.scalar.activation(sc8[:], up_bank[0][:, 0:E], ACT.Identity).then_inc(sc_copied, 1)
                            if g == 2 and h > 1:
                                tanh(p - 1, h - 2)
                            if g == 3 and h > 0:
                                tanh(p - 1, 1 + h)
                    if scores_here(p):
                        if g < 3:
                            copy_stack(p, g + 1)
                        elif next_here(p):
                            copy_stack(p + 1, 0)
                    if prev_here(p) and g == 2:
                        act.wait_ge(routed, p.times(ROUTES, -ROUTES + 1))
                        nc.scalar.activation(rt[:, 1:2], rt[:, 0:1], ACT.Exp).then_inc(dexp_done, 1)

            act.wait_ge(w_in, 16 * W_DMAS)
            nc.scalar.activation(tg[:], gts[:], ACT.Tanh).then_inc(tanh_g, 1)
            act.wait_ge(zeroed, 2)
            copy_stack(Pair(0), 0)
            bodies(act, body)

        @block.vector
        def _(dve):
            def ln_step(s, rooted, k, p, src, mid, agg, inv, dst):
                if k == 0:
                    nc.vector.bn_stats(mid[:], src).then_inc(s, 1)
                elif k == 1:
                    dve.wait_ge(s, p.times(3, 1))
                    settled(dve)
                    nc.vector.bn_aggr(agg[:], mid[:]).then_inc(s, 1)
                else:
                    dve.wait_ge(rooted, p.times(2, 2))
                    nc.vector.tensor_scalar(dst[:], src, agg[:, 0:1], inv[:, 0:1], ALU.subtract,
                                            ALU.mult).then_inc(s, 1)

            def norm_x(p, par, k):
                if k == 0:
                    dve.wait_ge(x_in[par], p.times(16, 32 - 16 * par))
                if k == 2:
                    if p.after(1, 0):
                        dve.wait_ge(q_proj, p.times(1, 0))
                ln_step(ln1, root1, k, p, xt[:, par, :], stats, mv, rstd, xn)

            def norm_x1(p, par, k):
                if k == 0:
                    dve.wait_ge(x1_done, p.times(1, 1))
                if k == 2:
                    if p.after(1, 0):
                        dve.wait_ge(x2_turned, p.times(1, 0))
                ln_step(ln2, root2, k, p, x1[:, par, :], stats2, mv2, rstd2, xn2)

            def rope(p, n):
                dve.wait_ge(q_proj if n == 0 else k_proj, p.times(1, 1))
                if p.after(3, -2):
                    dve.wait_ge(q_split if n == 0 else k_split, p.times(3, -2))
                nc.vector.scalar_tensor_tensor(rot_a[:, n, :], misc[:, 0:T], vec[:, 2 * n:2 * n + 1], cosT,
                                               ALU.add, ALU.mult)
                nc.vector.scalar_tensor_tensor(rot_b[:, n, :], misc[:, T:2 * T], vec[:, 2 * n + 1:2 * n + 2], sinT,
                                               ALU.add, ALU.mult).then_inc(q_roped if n == 0 else k_roped, 1)

            def copy_v(p, par):
                dve.wait_ge(v_proj, p.times(1, 1))
                if p.after(4, -4):
                    dve.wait_ge(pv_done, p.times(4, -4))
                nc.vector.tensor_tensor(vE[:, par, :, :, 0:KCH],
                                        misc[:, 0:T].rearrange("p (s h c) -> p s h c", s=TC, c=KCH), bvb[:],
                                        ALU.add).then_inc(v_copied, 1)

            def row_max(p, g, h):
                dve.wait_ge(scored, p.times(16, 4 * g + h + 1))
                nc.vector.tensor_reduce(negm[:, h, :], s_bank[h % 2][:].rearrange("p (t s) -> p t s", t=TC), AX.X,
                                        ALU.max, negate=True).then_inc(reduced, 1)

            def split_m(p, g, k):
                if k == 0:
                    dve.wait_ge(reduced, p.times(16, 4 * g + 4))
                    if p.after(4, g):
                        dve.wait_ge(m_turned, p.times(4, g))
                else:
                    dve.wait_ge(m_split, p.times(8, 2 * g + 1))
                hi = mpl[:, :, MROW::32]
                lo = mpl[:, :, MROW + 1::32]
                src = negm[:].rearrange("p h t -> p t h")
                if k == 0:
                    nc.vector.tensor_copy(hi, src).then_inc(m_split, 1)
                else:
                    nc.vector.tensor_tensor(lo, src, hi, ALU.subtract).then_inc(m_split, 1)

            def add_m(p, g):
                dve.wait_ge(m_turned, p.times(4, g + 1))
                if p.after(16, 4 * (g - 1)):
                    dve.wait_ge(scoredT, p.times(16, 4 * (g - 1)))
                nc.vector.tensor_tensor(qM[:, g % 2, :], st_bank[0][:, 0:T],
                                        qS[:, g % 2, :].bitcast(F32), ALU.add).then_inc(m_added, 1)

            def normalise(p, g, k):
                blocks = oT[:].rearrange("p (b r) -> p b r", r=32)
                if k == 0:
                    dve.wait_ge(pv_done, p.times(4, g - 1))
                    nc.vector.transpose(oT[:], pv_bank[:, (g % 2) * T:(g % 2) * T + T]).then_inc(turned_out, 1)
                elif k == 1:
                    dve.wait_ge(turned_out, p.times(4, g - 1))
                    nc.vector.reciprocal(rden[:], blocks[:, :, KCH:KCH + 1]).then_inc(inverted, 1)
                elif k == 2:
                    dve.wait_ge(inverted, p.times(4, g - 1))
                    nc.vector.tensor_tensor(blocks[:, :, 0:KCH], blocks[:, :, 0:KCH],
                                            rden[:].to_broadcast([P, T // 32, KCH]), ALU.mult).then_inc(divided, 1)
                else:
                    dve.wait_ge(divided, p.times(4, g - 1))
                    if p.after(1, -1):
                        dve.wait_ge(o_done, p.times(1, -1))
                    nc.vector.transpose(att[:, (g - 2) % GPP, :], oT[:]).then_inc(normed, 1)

            def glu_a(p, e):
                dve.wait_ge(tanh_done, p.times(8, e + 1))
                nc.vector.scalar_tensor_tensor(ug[:, e % 2, :], th[:, e % 2, :], 1.0, up_bank[e % 2][:, E:E + HID],
                                               ALU.add, ALU.mult).then_inc(u_done, 1)

            def glu_b(p, e):
                dve.wait_ge(u_done, p.times(8, e + 1))
                if e == 0:
                    dve.wait_ge(routed, p.times(ROUTES, ROUTES))
                    if p.after(3, 0):
                        dve.wait_ge(h_turned, p.times(3, 0))
                nc.vector.scalar_tensor_tensor(hid[:, e * HID:(e + 1) * HID], ug[:, e % 2, :], wts[:, e:e + 1],
                                               up_bank[e % 2][:, E + HID:E + UP], ALU.mult,
                                               ALU.mult).then_inc(h_done, 1)

            def body(p, par):
                for g in range(GPP):
                    for h in range(GH):
                        if norm_here(p, g) and h < 2:
                            normalise(p, g, 2 * h)
                        if scores_here(p):
                            row_max(p, g, h)
                        if norm_here(p, g) and h < 2:
                            normalise(p, g, 2 * h + 1)
                        if next_here(p) and h == 0 and g:
                            if g < 3:
                                rope(p + 1, g - 1)
                            else:
                                copy_v(p + 1, 1 - par)
                        if g == 0 and next_here(p) and h != 2:
                            norm_x(p + 1, 1 - par, min(h, 2))
                        if prev2_here(p):
                            if g == 0:
                                if h < 3 :
                                    if h == 0:
                                        glu_b(p - 2, 4)
                                if h > 0:
                                    glu_a(p - 2, 4 + h)
                                    glu_b(p - 2, 4 + h)
                            if g == 2 and h == 0:
                                dve.wait_ge(y_done, p.times(1, -1))
                                nc.vector.tensor_tensor(x1[:, par, :], up_bank[1][:, 0:T], x1[:, par, :],
                                                        ALU.add).then_inc(y_added, 1)
                        if prev_here(p):
                            if g == 1 and h == 2:
                                dve.wait_ge(o_done, p.times(1, 0))
                                dve.wait_ge(xres_done, p.times(1, 0))
                                if p.known and p.v >= 3:
                                    dve.wait_ge(stored[1 - par], (p - 3).times(8, 16 - 8 * (1 - par)))
                                nc.vector.scalar_tensor_tensor(x1[:, 1 - par, :], up_bank[0][:, 0:T], tg[:, 0:1],
                                                               xres[:, 1 - par, :], ALU.mult,
                                                               ALU.add).then_inc(x1_done, 1)
                            if g == 3:
                                if h == 0:
                                    glu_b(p - 1, 0)
                                elif h == 1:
                                    glu_b(p - 1, 1)
                                else:
                                    glu_a(p - 1, h)
                                    glu_b(p - 1, h)
                    if scores_here(p):
                        split_m(p, g, 0)
                    if g == 1 and prev_here(p):
                        norm_x1(p - 1, 1 - par, 0)
                    if g == 2 and prev_here(p):
                        dve.wait_ge(sc_copied, p.times(1, 0))
                        if p.after(ROUTES, -ROUTES):
                            dve.wait_ge(routed, p.times(ROUTES, -ROUTES))
                        settled(dve)
                        nc.vector.max(top8[:], sc8[:]).then_inc(top2, 1)
                    if scores_here(p):
                        split_m(p, g, 1)
                    if g == 1 and prev_here(p):
                        norm_x1(p - 1, 1 - par, 1)
                    if g == 2 and prev_here(p):
                        dve.wait_ge(top2, p.times(2, -1))
                        settled(dve)
                        nc.vector.max_index(idx8[:], top8[:], sc8[:]).then_inc(top2, 1)
                        glu_a(p - 1, 0)
                        glu_a(p - 1, 1)
                    if g == 3 and prev_here(p):
                        glu_a(p - 1, 4)
                    if scores_here(p):
                        add_m(p, g)
                    if g == 1 and prev_here(p):
                        norm_x1(p - 1, 1 - par, 2)

            nc.vector.memset(wp[:], 0.0)
            nc.vector.memset(wo[:], 0.0).then_inc(zeroed, 1)
            nc.vector.memset(mpl[:], 0.0)
            nc.vector.memset(vE[:], 1.0)
            nc.vector.memset(kM[:].bitcast(F32), 0.0).then_inc(zeroed, 1)
            dve.wait_ge(w_in, 16 * W_DMAS)
            for k in range(3):
                norm_x(Pair(0), 0, k)
            nc.vector.tensor_copy(sel_r[:], cst[:, C_SEL:C_SEL + 16 * P].rearrange("p (a b c) -> p a b c", a=4, b=GPP))
            nc.vector.tensor_copy(ident_b[:], ident).then_inc(consts_r, 1)
            dve.wait_ge(tanh_g, 1)
            nc.vector.tensor_scalar(tgo[:], vec[:, 4:5], tg[:, 0:1], None, ALU.mult)
            nc.vector.tensor_scalar(tgh[:], tg[:, 1:2], 0.5, None, ALU.mult).then_inc(gates_ready, 1)
            dve.wait_ge(zeroed, 2)
            rope(Pair(0), 0)
            rope(Pair(0), 1)
            copy_v(Pair(0), 0)
            bodies(dve, body)

        @block.gpsimd
        def _(pool):
            def split_qk(p, par, n):
                s = q_split if n == 0 else k_split
                pool.wait_ge(q_roped if n == 0 else k_roped, p.times(1, 1))
                nc.gpsimd.tensor_tensor(roped[:, n, :], rot_a[:, n, :], rot_b[:, n, :], ALU.add).then_inc(s, 1)
                pool.wait_ge(s, p.times(3, 1))
                if p.after(4, -4):
                    pool.wait_ge(stacked, p.times(4, -4))
                settled(pool)
                nc.gpsimd.tensor_copy(qk_hi[:, par, n, :], roped[:, n, :]).then_inc(s, 1)
                pool.wait_ge(s, p.times(3, 2))
                nc.gpsimd.tensor_tensor(qk_lo[:, par, n, :], roped[:, n, :], qk_hi[:, par, n, :].bitcast(F32),
                                        ALU.subtract).then_inc(s, 1)

            def residual(p, par):
                pool.wait_ge(x_in[par], p.times(16, 32 - 16 * par))
                if p.after(1, -1):
                    pool.wait_ge(x1_done, p.times(1, -1))
                settled(pool)
                nc.gpsimd.tensor_scalar(xres[:, par, :], xt[:, par, :], tgo[:, 0:1], None,
                                        ALU.add).then_inc(xres_done, 1)

            def inverse_root(p, s, done, agg, shifted, inv):
                pool.wait_ge(s, p.times(3, 2))
                settled(pool)
                nc.gpsimd.tensor_scalar(shifted[:], agg[:, 1:2], EPS, None, ALU.add).then_inc(done, 1)
                pool.wait_ge(done, p.times(2, 1))
                nc.gpsimd.tensor_tensor(inv[:], shifted[:], powers[:, 0:1], ALU.pow).then_inc(done, 1)

            def root_x(p):
                inverse_root(p, ln1, root1, mv, veps, rstd)

            def root_x1(p):
                inverse_root(p, ln2, root2, mv2, veps2, rstd2)

            def route(p):
                def step(k):
                    pool.wait_ge(routed, p.times(ROUTES, k))

                pool.wait_ge(top2, p.times(2, 2))
                nc.gpsimd.tensor_tensor(rt[:, 0:1], top8[:, 1:2], top8[:, 0:1], ALU.subtract).then_inc(routed, 1)
                settled(pool)
                nc.gpsimd.tensor_copy(idxf[:], idx8[:, 0:2]).then_inc(routed, 1)
                pool.wait_ge(dexp_done, p.times(1, 1))
                settled(pool)
                nc.gpsimd.tensor_scalar(rt[:, 5:6], rt[:, 1:2], 1.0, None, ALU.add).then_inc(routed, 1)
                step(3)
                nc.gpsimd.tensor_tensor(rt[:, 2:3], rt[:, 5:6], powers[:, 1:2], ALU.pow).then_inc(routed, 1)
                step(4)
                nc.gpsimd.tensor_tensor(rt[:, 3:4], tgh[:], rt[:, 2:3], ALU.mult).then_inc(routed, 1)
                step(5)
                nc.gpsimd.tensor_tensor(rt[:, 4:5], rt[:, 3:4], rt[:, 1:2], ALU.mult).then_inc(routed, 1)
                settled(pool)
                nc.gpsimd.tensor_scalar(oh[:, 0, :], iota8, idxf[:, 0:1], rt[:, 3:4], ALU.is_equal,
                                        ALU.mult).then_inc(routed, 1)
                step(6)
                settled(pool)
                nc.gpsimd.tensor_scalar(oh[:, 1, :], iota8, idxf[:, 1:2], rt[:, 4:5], ALU.is_equal,
                                        ALU.mult).then_inc(routed, 1)
                step(8)
                if p.after(8, 0):
                    pool.wait_ge(h_done, p.times(8, 0))
                nc.gpsimd.tensor_tensor(wts[:], oh[:, 0, :], oh[:, 1, :], ALU.add).then_inc(routed, 1)

            def body(p, par):
                if next_here(p):
                    root_x(p + 1)
                    split_qk(p + 1, 1 - par, 0)
                if prev_here(p):
                    root_x1(p - 1)
                if next_here(p):
                    split_qk(p + 1, 1 - par, 1)
                if prev_here(p):
                    route(p - 1)
                if next_here(p):
                    residual(p + 1, 1 - par)

            nc.gpsimd.memset(powers[:, 0:1], -0.5)
            nc.gpsimd.memset(powers[:, 1:2], -1.0).then_inc(pool_consts, 1)
            pool.wait_ge(pool_consts, 1)
            root_x(Pair(0))
            pool.wait_ge(gates_ready, 1)
            split_qk(Pair(0), 0, 0)
            split_qk(Pair(0), 0, 1)
            residual(Pair(0), 0)
            bodies(pool, body)


_OUTS = [((B, C, T), "float32")]


def kernel(**inputs):
    import numpy as _np
    import concourse.bacc as _bacc
    from concourse import mybir as _mybir
    from concourse.bass_utils import run_bass_kernel_spmd as _run

    a = {k: _np.asarray(v) for k, v in inputs.items()}
    turn = _np.arange(C).reshape(HEADS, 2, KCH // 2)[:, ::-1, :].reshape(C)
    wq, wk, wv = (a["L0_xattn_W" + n] for n in "qkv")
    bq, bk, bo = (a["L0_xattn_b" + n] for n in "qko")
    w_proj = _np.concatenate([wq.T, wq[turn].T, wk.T, wk[turn].T, wv.T], axis=1)
    vecs = _np.stack([_np.concatenate([v, v]) for v in (bq, bq[turn], bk, bk[turn], bo)], axis=1)
    bv = _np.concatenate([a["L0_xattn_bv"]] * (2 * TC))[None, :]
    gates = _np.concatenate([a["g_xattn"], a["g_ffn"]])[None, :]
    up = _np.concatenate([a["L0_ffn_W1"], a["L0_ffn_W2"]], axis=1).reshape(E * UP, T)
    w_up = _np.concatenate([a["L0_ffn_Wg"], up], axis=0).T
    w_down = a["L0_ffn_W3"].transpose(0, 2, 1).reshape(E * HID, T)
    given = {"x": a["x"], "ctx": a["ctx_2048"], "w_proj": w_proj, "w_o": a["L0_xattn_Wo"].T, "vecs": vecs, "bv": bv,
             "gates": gates, "w_up": w_up, "w_down": w_down, "const": constants()}

    nc = _bacc.Bacc("TRN2", target_bir_lowering=False, num_devices=1)
    arrays, args = {}, []
    for name, v in given.items():
        v = _np.ascontiguousarray(v)
        arrays[f"in_{name}_dram"] = v
        args.append(nc.dram_tensor(f"in_{name}_dram", v.shape, _mybir.dt.from_np(v.dtype), kind="ExternalInput").ap())
    for i, (shape, dtype) in enumerate(_OUTS):
        dt = _mybir.dt.from_np(_np.dtype(dtype))
        args.append(nc.dram_tensor(f"out_{i}_dram", shape, dt, kind="ExternalOutput").ap())
    build(nc, *args)
    r = _run(nc, [arrays], core_ids=[0])
    return r.results[0]["out_0_dram"]
```

```python
from contextlib import ExitStack

import numpy as np

import concourse.bass as bass
from concourse import mybir

F32 = mybir.dt.float32
F32R = mybir.dt.float32r
BF16 = mybir.dt.bfloat16
U32 = mybir.dt.uint32
ALU = mybir.AluOpType
ACT = mybir.ActivationFunctionType
AX = mybir.AxisListType

B, C, T = 32, 64, 256
HEADS, KCH = 8, 8
E, HID = 8, 176
P = 128
PAIRS = B // 2
GH = 4
GPP = 2 * HEADS // GH
GROUPS = PAIRS * GPP
TC = T // P
SCALE = float(KCH) ** -0.5
EPS = 1e-5
FCH = E * HID // P
UP = 2 * HID
ROUTES = 7
SPLITS = 6
PIECE = (E + E * UP) // 2
MROW = 3 * KCH

C_COS, C_SIN, C_SEL, C_ID, C_ONE, C_IOTA = 0, T, 2 * T, 2 * T + 16 * P, 2 * T + 17 * P, 2 * T + 17 * P + 1
C_ALL = C_IOTA + E


def constants():
    inv = np.float32(1.0) / np.power(np.float32(10000.0), np.arange(0, KCH, 2, dtype=np.float32) / np.float32(KCH))
    f = np.arange(T, dtype=np.float32)[:, None] * inv.astype(np.float32)[None, :]
    f = np.concatenate([f, f], axis=-1)
    sign = np.where(np.arange(KCH) < KCH // 2, -1.0, 1.0).astype(np.float32)
    out = np.zeros((P, C_ALL), np.float32)
    out[:, C_COS:C_COS + T] = np.tile(np.cos(f).T, (P // KCH, 1))
    out[:, C_SIN:C_SIN + T] = np.tile((np.sin(f) * sign).T, (P // KCH, 1))
    rows = ((0, 1), (2,), (0, 2), (1,))
    sel = np.zeros((P, 4, GPP, P), np.float32)
    for kind in range(4):
        for g in range(GPP):
            for j in range(GH):
                for r in rows[kind]:
                    for c in range(KCH):
                        sel[g * GH * KCH + j * KCH + c, kind, g, 32 * j + r * KCH + c] = 1.0
    out[:, C_SEL:C_SEL + 16 * P] = sel.reshape(P, 16 * P)
    out[:, C_ID:C_ID + P] = np.eye(P, dtype=np.float32)
    for j in range(GH):
        out[32 * j + MROW:32 * j + MROW + 2, C_ONE] = 1.0
    out[:, C_IOTA:C_IOTA + E] = np.arange(E, dtype=np.float32)
    return out


class Pair:

    def __init__(self, v, least=None):
        self.v, self.least, self.known = v, least, least is None

    def __add__(self, n):
        return Pair(self.v + n, None if self.known else self.least + n)

    def __sub__(self, n):
        return Pair(self.v - n, None if self.known else self.least - n)

    def times(self, per, plus):
        assert (per * self.v if self.known else per * self.least) + plus > 0
        return self.v * per + plus if plus else self.v * per

    def after(self, per, plus):
        if self.known:
            return per * self.v + plus > 0
        assert per * self.least + plus > 0
        return True


def build(nc, x, ctx_in, w_proj, w_o, vecs, bv, gates, w_up, w_down, const, out):
    x_d = x.rearrange("(n b) c t -> n (b c) t", b=2)
    c_d = ctx_in.rearrange("(n b) c t -> n (b c) t", b=2)
    o_d = out.rearrange("(n b) c t -> n (b c) t", b=2)

    with ExitStack() as stack:
        def sb(name, shape, dt=F32):
            return stack.enter_context(nc.sbuf_tensor(name, shape, dt))

        def bank(name):
            return stack.enter_context(nc.psum_tensor(name, [P, 512], F32))

        def sem(name):
            return stack.enter_context(nc.semaphore(name))

        cst = sb("cst", [P, C_ALL])
        cosT, sinT = cst[:, C_COS:C_COS + T], cst[:, C_SIN:C_SIN + T]
        ident = cst[:, C_ID:C_ID + P]
        m_rows_one = cst[:, C_ONE:C_ONE + 1]
        iota8 = cst[:, C_IOTA:C_IOTA + E]
        sel_r = sb("sel_r", [P, 4, GPP, P], F32R)
        ident_b = sb("ident_b", [P, P], BF16)
        wp = sb("wp", [P, 5, P])
        wo = sb("wo", [P, 2, C])
        vec = sb("vec", [P, 5])
        bvb = sb("bvb", [P, TC, 2 * HEADS, KCH])
        gts = sb("gts", [P, 2])
        tg = sb("tg", [P, 2])
        tgo = sb("tgo", [P, 1])
        tgh = sb("tgh", [P, 1])
        w_stage = sb("w_stage", [P, 2, PIECE])
        wup_lo = sb("wup_lo", [P, 2, E + E * UP], F32R)
        wdn_lo = sb("wdn_lo", [P, FCH, T], F32R)
        wup_hi = sb("wup_hi", [P, 2, E + E * UP], F32R)
        wdn_hi = sb("wdn_hi", [P, FCH, T], F32R)
        xt = sb("xt", [P, 2, T])
        ct = sb("ct", [P, 2, T])
        stats = sb("stats", [P, 6])
        mv = sb("mv", [P, 2])
        rstd = sb("rstd", [P, 1])
        shift = sb("shift", [P, 1])
        xn = sb("xn", [P, T])
        rot_a = sb("rot_a", [P, 2, T])
        rot_b = sb("rot_b", [P, 2, T])
        roped = sb("roped", [P, 2, T])
        qk_hi = sb("qk_hi", [P, 2, 2, T], F32R)
        qk_lo = sb("qk_lo", [P, 2, 2, T], F32R)
        vE = sb("vE", [P, 2, TC, 2 * HEADS, 32])
        xres = sb("xres", [P, 2, T])
        qS = sb("qS", [P, GPP, T], F32R)
        kM = sb("kM", [P, GPP, GH, T], F32R)
        qM = sb("qM", [P, 2, T], F32R)
        negm = sb("negm", [P, GH, TC])
        mpl = sb("mpl", [P, TC, P], BF16)
        probs = sb("probs", [P, 2, GH, TC, T])
        powers = sb("powers", [P, 2])
        veps, veps2 = sb("veps", [P, 1]), sb("veps2", [P, 1])
        oT = sb("oT", [P, T])
        rden = sb("rden", [P, T // 32, 1])
        att = sb("att", [P, GPP, T])
        x1 = sb("x1", [P, 2, T])
        stats2 = sb("stats2", [P, 6])
        mv2 = sb("mv2", [P, 2])
        rstd2 = sb("rstd2", [P, 1])
        xn2 = sb("xn2", [P, T])
        xT2_hi = sb("xT2_hi", [P, 2, P], F32R)
        xT2_lo = sb("xT2_lo", [P, 2, P], F32R)
        sc8 = sb("sc8", [P, E])
        top8 = sb("top8", [P, 8])
        idx8 = sb("idx8", [P, 8], U32)
        idxf = sb("idxf", [P, 2])
        rt = sb("rt", [P, 8])
        oh = sb("oh", [P, 2, E])
        wts = sb("wts", [P, E])
        th = sb("th", [P, 2, HID])
        ug = sb("ug", [P, 2, HID])
        hid = sb("hid", [P, E * HID])
        hT_hi = sb("hT_hi", [P, FCH, P], F32R)
        hT_lo = sb("hT_lo", [P, FCH, P], F32R)

        s_bank = [bank("s_bank0"), bank("s_bank1")]
        st_bank = [bank("st_bank0"), bank("st_bank1")]
        pv_bank = bank("pv_bank")
        up_bank = [bank("up_bank0"), bank("up_bank1")]
        misc = bank("misc")
        turned_bank = (misc, up_bank[0], up_bank[1])

        proj_in, tables_in, consts_in = sem("proj_in"), sem("tables_in"), sem("consts_in")
        small_in, experts_in = sem("small_in"), [sem("experts_in0"), sem("experts_in1")]
        x_in = [sem("x_in0"), sem("x_in1")]
        stored = [sem("stored0"), sem("stored1")]
        zeroed = sem("zeroed")
        waits_over = sem("waits_over")
        tanh_g = sem("tanh_g")
        gates_ready = sem("gates_ready")
        consts_r = sem("consts_r")
        q_proj, k_proj, v_proj = sem("q_proj"), sem("k_proj"), sem("v_proj")
        stacked, scored, scoredT = sem("stacked"), sem("scored"), sem("scoredT")
        m_turned, pv_done, o_done = sem("m_turned"), sem("pv_done"), sem("o_done")
        x2_turned, up_done, h_turned, y_done = sem("x2_turned"), sem("up_done"), sem("h_turned"), sem("y_done")
        stack_copied, exp_done = sem("stack_copied"), sem("exp_done")
        x_normed = sem("x_normed")
        x2_copied, sc_copied, tanh_done = sem("x2_copied"), sem("sc_copied"), sem("tanh_done")
        h_copied, dexp_done, w_rounded = sem("h_copied"), sem("dexp_done"), sem("w_rounded")
        ln1, ln2 = sem("ln1"), sem("ln2")
        q_roped, k_roped, v_copied = sem("q_roped"), sem("k_roped"), sem("v_copied")
        reduced, m_split, m_added = sem("reduced"), sem("m_split"), sem("m_added")
        turned_out, inverted, divided, normed, x1_done = sem("turned_out"), sem("inverted"), sem("divided"), sem("normed"), sem("x1_done")
        x2_split, h_split, w_split = sem("x2_split"), sem("h_split"), sem("w_split")
        top2, u_done, h_done, y_added = sem("top2"), sem("u_done"), sem("h_done"), sem("y_added")
        root1, root2, pool_consts = sem("root1"), sem("root2"), sem("pool_consts")
        q_split, k_split, xres_done, routed = sem("q_split"), sem("k_split"), sem("xres_done"), sem("routed")

        SMALL_DMAS = 2 + HEADS

        LOOP_FROM = 2
        LOOP_TO = PAIRS - 2

        def settled(eng):
            eng.sem_inc(waits_over, 1)

        def bodies(eng, body):
            body(Pair(0), 0)
            body(Pair(1), 1)
            with eng.Fori(LOOP_FROM // 2, LOOP_TO // 2) as i:
                body(Pair(i * 2, LOOP_FROM), 0)
                body(Pair(i * 2 + 1, LOOP_FROM + 1), 1)
            for p in range(LOOP_TO, PAIRS + 2):
                body(Pair(p), p % 2)

        def at(p, low, high):
            if p.known:
                return low <= p.v <= high
            assert low <= LOOP_FROM and high >= LOOP_TO - 1
            return True

        def piece(tile, n):
            if n < 4:
                return tile[0][:, n // 2, (n % 2) * PIECE:(n % 2 + 1) * PIECE]
            return tile[1].rearrange("p k n -> p (k n)")[:, (n - 4) * FCH * T // 2:(n - 3) * FCH * T // 2]

        def staged(n):
            return w_stage[:, n % 2, 0:PIECE if n < 4 else FCH * T // 2]

        def scores_here(p):
            return at(p, 0, PAIRS - 1)

        def before_here(p, g):
            return at(p, 0 if g else 1, PAIRS if g == 0 else PAIRS - 1)

        def norm_here(p, g):
            return at(p, 0 if g > 1 else 1, PAIRS if g < 2 else PAIRS - 1)

        def next_here(p):
            return at(p, 0, PAIRS - 2)

        def prev_here(p):
            return at(p, 1, PAIRS)

        def prev2_here(p):
            return at(p, 2, PAIRS + 1)

        block = stack.enter_context(nc.Block())

        @block.sync
        def _(sp):
            def load(p, par):
                if p.after(1, -1):
                    sp.wait_ge(xres_done, p.times(1, -1))
                    settled(sp)
                if p.after(1, -1):
                    sp.wait_ge(x_normed, p.times(1, -1))
                    settled(sp)
                if p.after(1, -1):
                    sp.wait_ge(v_proj, p.times(1, -1))
                    settled(sp)
                sp.dma_start(xt[:, par, :], x_d[p.v, :, :]).then_inc(x_in[par], 16)
                sp.dma_start(ct[:, par, :], c_d[p.v, :, :]).then_inc(x_in[par], 16)

            load(Pair(0), 0)
            sp.dma_start(vec[:], vecs).then_inc(proj_in, 16)
            sp.wait_ge(zeroed, 1)
            for b in range(2):
                sp.dma_start(wp[b * C:(b + 1) * C, :, b * C:(b + 1) * C],
                             w_proj.rearrange("c (n o) -> c n o", n=5)).then_inc(proj_in, 16)
            sp.dma_start(cst[:, 0:C_SEL], const[:, 0:C_SEL]).then_inc(tables_in, 16)
            sp.dma_start(gts[:], gates.to_broadcast([P, 2])).then_inc(small_in, 16)
            sp.dma_start(bvb[:].rearrange("p s h c -> p (s h c)"), bv.to_broadcast([P, TC * 2 * C])).then_inc(small_in, 16)
            sp.dma_start(cst[:, C_SEL:C_ALL], const[:, C_SEL:C_ALL]).then_inc(consts_in, 16)
            load(Pair(1), 1)
            sp.wait_ge(zeroed, 2)
            for h in range(HEADS):
                g, j = divmod(h, GH)
                sp.dma_start(wo[32 * j:32 * j + KCH, g, :], w_o[h * KCH:(h + 1) * KCH, :]).then_inc(small_in, 16)
            w_d = (w_up.rearrange("(k p) n -> p k n", p=P), w_down)
            for n in range(SPLITS):
                if n >= 2:
                    sp.wait_ge(w_split, n - 1)
                sp.dma_start(staged(n), piece(w_d, n)).then_inc(experts_in[n % 2], 16)

            def body(p, par):
                if prev2_here(p):
                    sp.wait_ge(y_added, p.times(1, -1))
                    settled(sp)
                    sp.dma_start(o_d[(p - 2).v, :, :], x1[:, par, :]).then_inc(stored[par], 16)
                if at(p, 0, PAIRS - 3):
                    if prev2_here(p):
                        sp.wait_ge(stored[par], (p - 2).times(8, 16 - 8 * (par)))
                        settled(sp)
                    load(p + 2, par)

            bodies(sp, body)
            sp.wait_ge(stored[0], 16 * (PAIRS // 2))
            sp.wait_ge(stored[1], 16 * (PAIRS // 2))

        @block.tensor
        def _(pe):
            def score(p, g, h):
                G4 = 4 * g + h
                if h == 0:
                    pe.wait_ge(stack_copied, p.times(4, g + 1))
                if p.after(16, G4 - 1):
                    pe.wait_ge(reduced, p.times(16, G4 - 1))
                for t in range(TC):
                    mm = pe.matmul(s_bank[h % 2][:, t * T:(t + 1) * T], qS[:, g, t * P:(t + 1) * P],
                                   kM[:, g, h, :], start=True, stop=True)
                mm.then_inc(scored, 1)

            def score_t(p, g, h):
                n = 4 * (g - 1) + h
                if h == 0:
                    pe.wait_ge(m_added, p.times(4, g))
                if p.after(16, n - 1):
                    pe.wait_ge(exp_done, p.times(16, n - 1))
                for s in range(TC):
                    mm = pe.matmul(st_bank[h % 2][:, s * T:(s + 1) * T],
                                   kM[:, (g - 1) % GPP, h, s * P:(s + 1) * P], qM[:, (g - 1) % 2, :],
                                   start=True, stop=True)
                mm.then_inc(scoredT, 1)

            def weigh(p, g):
                par = (g - 1) % 2
                vpar = PARITY[0] if g else 1 - PARITY[0]
                gg = (g - 1) % GPP
                pe.wait_ge(exp_done, p.times(16, 4 * g))
                if p.after(4, g - 1):
                    pe.wait_ge(turned_out, p.times(4, g - 1))
                for s in range(TC):
                    for j in range(GH):
                        mm = pe.matmul(pv_bank[32 * j:32 * j + 32, (gg % 2) * T:(gg % 2) * T + T],
                                       vE[:, vpar, s, gg * GH + j, :], probs[:, par, j, s, :],
                                       start=(s == 0), stop=(s == TC - 1))
                mm.then_inc(pv_done, 1)

            def turn_m(p, g):
                pe.wait_ge(m_split, p.times(8, 2 * g + 2))
                if p.after(16, 4 * g - 1):
                    pe.wait_ge(exp_done, p.times(16, 4 * g - 1))
                for t in range(TC):
                    mm = pe.matmul(st_bank[0][:, t * P:(t + 1) * P], mpl[:, t, :], ident_b[:],
                                   start=True, stop=True)
                mm.then_inc(m_turned, 1)

            def stack_qk(p, g, par):
                if g == 0:
                    pe.wait_ge(q_split, p.times(3, 3))
                    pe.wait_ge(k_split, p.times(3, 3))
                for n in range(2):
                    for part, src in enumerate((qk_hi, qk_lo)):
                        mm = pe.matmul(misc[:, n * T:(n + 1) * T], sel_r[:, 2 * n + part, g, :], src[:, par, n, :],
                                       start=(part == 0), stop=(part == 1))
                mm.then_inc(stacked, 1)

            def project(p, par, n):
                src = xn[:] if n == 0 else ct[:, par, :]
                if n == 0:
                    pe.wait_ge(x_normed, p.times(1, 1))
                else:
                    pe.wait_ge(x_in[par], p.times(16, 32 - 16 * par))
                for r in range(2):
                    mm = pe.matmul(misc[:, r * T:(r + 1) * T], wp[:, 2 * n + r, :], src, start=True, stop=True)
                mm.then_inc(q_proj if n == 0 else k_proj, 1)

            def project_v(p, par):
                for s in range(TC):
                    mm = pe.matmul(misc[:, s * P:(s + 1) * P], ct[:, par, s * P:(s + 1) * P], wp[:, 4, :],
                                   start=True, stop=True)
                mm.then_inc(v_proj, 1)

            def project_o(p):
                pe.wait_ge(normed, p.times(4, 4))
                if p.after(3, -1):
                    pe.wait_ge(h_split, p.times(3, -1))
                for g in range(2):
                    for b in range(2):
                        mm = pe.matmul(up_bank[0][b * C:(b + 1) * C, 0:T], wo[:, g, :], att[:, 2 * b + g, :],
                                       start=(g == 0), stop=(g == 1))
                mm.then_inc(o_done, 1)

            def turn_x2(p):
                pe.wait_ge(ln2, p.times(3, 3))
                for k in range(2):
                    mm = pe.transpose(up_bank[0][:, k * P:(k + 1) * P], xn2[:, k * P:(k + 1) * P], ident)
                mm.then_inc(x2_turned, 1)

            def up(p, e):
                if e == 0:
                    pe.wait_ge(x2_split, p.times(1, 1))
                    if p.known and p.v == 0:
                        pe.wait_ge(w_split, SPLITS)
                if e == 1 and p.after(1, 0):
                    pe.wait_ge(y_added, p.times(1, 0))
                if e > 1:
                    pe.wait_ge(h_done, p.times(8, e - 1))
                cols = slice(0, E + UP) if e == 0 else slice(E + e * UP, E + (e + 1) * UP)
                at_ = 0 if e == 0 else E
                parts = ((xT2_hi, wup_hi[:]), (xT2_hi, wup_lo[:]), (xT2_lo, wup_hi[:]))
                for n, (a, w) in enumerate(parts):
                    for k in range(2):
                        mm = pe.matmul(up_bank[e % 2][:, at_:E + UP], a[:, k, :], w[:, k, cols],
                                       start=(n == 0 and k == 0), stop=(n == 2 and k == 1))
                mm.then_inc(up_done, 1)

            def turn_h(p, r):
                if r == 0:
                    pe.wait_ge(h_done, p.times(8, 3))
                    if p.known and p.v + 2 < PAIRS or not p.known:
                        pe.wait_ge(stack_copied, p.times(4, 10))
                else:
                    pe.wait_ge(h_done, p.times(8, 6 + r))
                for k in range(4 * r, min(4 * r + 4, FCH)):
                    mm = pe.transpose(turned_bank[r][:, (k % 4) * P:(k % 4 + 1) * P], hid[:, k * P:(k + 1) * P], ident)
                mm.then_inc(h_turned, 1)

            def down(p, low, high):
                if low == 0:
                    pe.wait_ge(h_split, p.times(3, 3))
                for k in range(low, high):
                    for n, (a, w) in enumerate(((hT_hi, wdn_hi[:]), (hT_hi, wdn_lo[:]), (hT_lo, wdn_hi[:]))):
                        mm = pe.matmul(up_bank[1][:, 0:T], a[:, k, :], w[:, k, :],
                                       start=(k == 0 and n == 0), stop=(k == FCH - 1 and n == 2))
                if high == FCH:
                    mm.then_inc(y_done, 1)

            PARITY = [0]

            def stack_next(p, g, par):
                if g == 0:
                    pe.wait_ge(stack_copied, p.times(4, 1))
                    stack_qk(p, 1, par)
                elif g < 3:
                    if not next_here(p):
                        pe.wait_ge(stack_copied, p.times(4, g + 1))
                        if g == 1:
                            pe.wait_ge(h_split, p.times(3, -5))
                    elif g == 1:
                        pe.wait_ge(q_roped, p.times(1, 2))
                    else:
                        pe.wait_ge(k_roped, p.times(1, 2))
                    stack_qk(p, g + 1, par)
                elif next_here(p):
                    pe.wait_ge(v_copied, p.times(1, 2))
                    stack_qk(p + 1, 0, 1 - par)

            def body(p, par):
                PARITY[0] = par
                for g in range(GPP):
                    for h in range(GH):
                        if scores_here(p) and g and h == 2 and g < 3:
                            stack_next(p, g, par)
                        if prev_here(p) and (g, h) == (2, 1):
                            turn_x2(p - 1)
                        if scores_here(p):
                            score(p, g, h)
                        if before_here(p, g):
                            score_t(p, g, h)
                        if scores_here(p) and (g, h) in ((0, 0), (3, 1)):
                            stack_next(p, g, par)
                        if next_here(p) and h == 0 and g:
                            if g == 1 and prev2_here(p):
                                pe.wait_ge(h_split, p.times(3, -5))
                            else:
                                pe.wait_ge(stack_copied, p.times(4, g + 1))
                            if g < 3:
                                project(p + 1, 1 - par, g - 1)
                            else:
                                project_v(p + 1, 1 - par)
                        if prev2_here(p):
                            if g == 0 and h < 2:
                                up(p - 2, 5 + h)
                            if g == 0 and h == 2:
                                turn_h(p - 2, 0)
                            if g == 0 and h == 3:
                                up(p - 2, 7)
                            if g == 1 and h < 2:
                                turn_h(p - 2, 1 + h)
                        if prev_here(p):
                            if g == 1 and h == 2:
                                project_o(p - 1)
                        if prev2_here(p):
                            if g == 1 and h == 2:
                                down(p - 2, 0, 3)
                            if g == 1 and h == 3:
                                down(p - 2, 3, 7)
                            if g == 2 and h == 0:
                                down(p - 2, 7, FCH)
                        if prev_here(p):
                            if g == 2 and h > 1:
                                up(p - 1, h - 2)
                            if g == 3 and h > 0:
                                up(p - 1, 1 + h)
                    if scores_here(p):
                        turn_m(p, g)
                    if before_here(p, g):
                        weigh(p, g)

            pe.wait_ge(proj_in, 16 * 3)
            pe.wait_ge(zeroed, 1)
            project(Pair(0), 0, 0)
            pe.wait_ge(q_roped, 1)
            project(Pair(0), 0, 1)
            pe.wait_ge(k_roped, 1)
            project_v(0, 0)
            pe.wait_ge(v_copied, 1)
            pe.wait_ge(consts_r, 1)
            stack_qk(Pair(0), 0, 0)
            pe.wait_ge(small_in, 16 * SMALL_DMAS)
            bodies(pe, body)

        @block.scalar
        def _(act):
            def expo(p, g, h):
                n = 4 * (g - 1) + h
                act.wait_ge(scoredT, p.times(16, n + 1))
                if p.after(4, g - 2):
                    act.wait_ge(pv_done, p.times(4, g - 2))
                nc.scalar.activation(probs[:, (g - 1) % 2, h, :, :].rearrange("p s t -> p (s t)"), st_bank[h % 2][:],
                                     ACT.Exp, scale=SCALE).then_inc(exp_done, 1)

            def copy_stack(p, g, half):
                if half == 0:
                    act.wait_ge(stacked, p.times(4, g + 1))
                    if p.after(16, 4 * (g - 3)):
                        act.wait_ge(scoredT, p.times(16, 4 * (g - 3)))
                    nc.scalar.activation(qS[:, g, :], misc[:, 0:T], ACT.Identity)
                for j in range(2 * half, 2 * half + 2):
                    rows = slice(32 * j, 32 * j + 32)
                    last = nc.scalar.activation(kM[rows, g, j, :], misc[rows, T:2 * T], ACT.Identity,
                                                bias=m_rows_one[rows, :])
                if half == 1:
                    last.then_inc(stack_copied, 1)

            def copy_next(p, g, half):
                if g < 3:
                    copy_stack(p, g + 1, half)
                elif next_here(p):
                    copy_stack(p + 1, 0, half)

            def copy_h(p, r):
                act.wait_ge(h_turned, p.times(3, r + 1))
                n = min(4, FCH - 4 * r) * P
                nc.scalar.activation(hT_hi[:, 4 * r:4 * r + n // P, :].rearrange("p k t -> p (k t)"),
                                     turned_bank[r][:, 0:n], ACT.Identity).then_inc(h_copied, 1)

            def norm_x(p, par):
                act.wait_ge(root1, p.times(3, 3))
                if p.after(1, 0):
                    act.wait_ge(q_proj, p.times(1, 0))
                nc.scalar.activation(xn[:], xt[:, par, :], ACT.Identity, scale=rstd[:, 0:1],
                                     bias=shift[:, 0:1]).then_inc(x_normed, 1)

            def tanh(p, e):
                act.wait_ge(up_done, p.times(8, e + 1))
                if p.after(8, e - 1):
                    act.wait_ge(u_done, p.times(8, e - 1))
                nc.scalar.activation(th[:, e % 2, :], up_bank[e % 2][:, E:E + HID], ACT.Tanh,
                                     scale=0.5).then_inc(tanh_done, 1)

            def body(p, par):
                for g in range(GPP):
                    for h in range(GH):
                        if prev_here(p) and g == 3 and h == 0:
                            tanh(p - 1, 1)
                        if prev_here(p) and (g, h) == (2, 1):
                            act.wait_ge(x2_turned, p.times(1, 0))
                            if p.after(8, -8):
                                act.wait_ge(up_done, p.times(8, -8))
                            nc.scalar.activation(xT2_hi[:].rearrange("p k t -> p (k t)"), up_bank[0][:, 0:2 * P],
                                                 ACT.Identity).then_inc(x2_copied, 1)
                        if prev_here(p) and g == 2 and h == 3:
                            act.wait_ge(up_done, p.times(8, -7))
                            if p.after(2, -2):
                                act.wait_ge(top2, p.times(2, -2))
                            nc.scalar.activation(sc8[:], up_bank[0][:, 0:E], ACT.Identity).then_inc(sc_copied, 1)
                        if scores_here(p) and g and h == 2:
                            copy_next(p, g, 0)
                        if before_here(p, g):
                            expo(p, g, h)
                        if scores_here(p) and g and h == 3:
                            copy_next(p, g, 1)
                        if scores_here(p) and (g, h) == (0, 1):
                            copy_next(p, g, 0)
                            copy_next(p, g, 1)
                        if prev_here(p) and (g, h) == (2, 3):
                            tanh(p - 1, 0)
                        if prev2_here(p) and (g, h) == (0, 3):
                            tanh(p - 2, 7)
                        if next_here(p) and (g, h) == (0, 3):
                            norm_x(p + 1, 1 - par)
                        if prev2_here(p):
                            if g == 0 and h < 2:
                                tanh(p - 2, 5 + h)
                            if g == 0 and h == 3:
                                copy_h(p - 2, 0)
                            if g == 1 and h < 2:
                                copy_h(p - 2, 1 + h)
                        if prev_here(p):
                            if g == 3 and h > 0:
                                tanh(p - 1, 1 + h)
                        if p.known and p.v == 0 and 4 <= 4 * g + h < 4 + SPLITS:
                            n = 4 * g + h - 4
                            act.wait_ge(experts_in[n % 2], 16 * (n // 2 + 1))
                            nc.scalar.activation(piece((wup_hi[:], wdn_hi[:]), n), staged(n),
                                                 ACT.Identity).then_inc(w_rounded, 1)
                    if prev_here(p) and g == 2:
                        act.wait_ge(top2, p.times(2, -1))
                        if p.after(ROUTES, -ROUTES):
                            act.wait_ge(routed, p.times(ROUTES, -ROUTES))
                        nc.scalar.activation(rt[:, 0:1], top8[:, 0:1], ACT.Exp, scale=-1.0,
                                             bias=top8[:, 1:2]).then_inc(dexp_done, 1)

            norm_x(Pair(0), 0)
            act.wait_ge(small_in, 16 * SMALL_DMAS)
            nc.scalar.activation(tg[:], gts[:], ACT.Tanh).then_inc(tanh_g, 1)
            act.wait_ge(consts_in, 16)
            act.wait_ge(zeroed, 4)
            copy_stack(Pair(0), 0, 0)
            copy_stack(Pair(0), 0, 1)
            bodies(act, body)

        @block.vector
        def _(dve):
            def ln_step(s, rooted, k, steps, p, src, mid, agg, inv, dst):
                if k == 0:
                    nc.vector.bn_stats(mid[:], src).then_inc(s, 1)
                elif k == 1:
                    dve.wait_ge(s, p.times(steps, 1))
                    settled(dve)
                    nc.vector.bn_aggr(agg[:], mid[:]).then_inc(s, 1)
                else:
                    dve.wait_ge(rooted, p.times(2, 2))
                    nc.vector.tensor_scalar(dst[:], src, agg[:, 0:1], inv[:, 0:1], ALU.subtract,
                                            ALU.mult).then_inc(s, 1)

            def norm_x(p, par, k):
                if k == 0:
                    dve.wait_ge(x_in[par], p.times(16, 32 - 16 * par))
                ln_step(ln1, None, k, 2, p, xt[:, par, :], stats, mv, None, None)

            def norm_x1(p, par, k):
                if k == 0:
                    dve.wait_ge(x1_done, p.times(1, 1))
                if k == 2:
                    if p.after(1, 0):
                        dve.wait_ge(x2_turned, p.times(1, 0))
                ln_step(ln2, root2, k, 3, p, x1[:, par, :], stats2, mv2, rstd2, xn2)

            def rope(p, n):
                dve.wait_ge(q_proj if n == 0 else k_proj, p.times(1, 1))
                if p.after(3, -2):
                    dve.wait_ge(q_split if n == 0 else k_split, p.times(3, -2))
                nc.vector.scalar_tensor_tensor(rot_a[:, n, :], misc[:, 0:T], vec[:, 2 * n:2 * n + 1], cosT,
                                               ALU.add, ALU.mult)
                nc.vector.scalar_tensor_tensor(rot_b[:, n, :], misc[:, T:2 * T], vec[:, 2 * n + 1:2 * n + 2], sinT,
                                               ALU.add, ALU.mult).then_inc(q_roped if n == 0 else k_roped, 1)

            def copy_v(p, par):
                dve.wait_ge(v_proj, p.times(1, 1))
                if p.after(4, -4):
                    dve.wait_ge(pv_done, p.times(4, -4))
                nc.vector.tensor_tensor(vE[:, par, :, :, 0:KCH],
                                        misc[:, 0:T].rearrange("p (s h c) -> p s h c", s=TC, c=KCH), bvb[:],
                                        ALU.add).then_inc(v_copied, 1)

            def row_max(p, g, h):
                dve.wait_ge(scored, p.times(16, 4 * g + h + 1))
                nc.vector.tensor_reduce(negm[:, h, :], s_bank[h % 2][:].rearrange("p (t s) -> p t s", t=TC), AX.X,
                                        ALU.max, negate=True).then_inc(reduced, 1)

            def split_m(p, g, k):
                if k == 0:
                    dve.wait_ge(reduced, p.times(16, 4 * g + 4))
                    if p.after(4, g):
                        dve.wait_ge(m_turned, p.times(4, g))
                else:
                    dve.wait_ge(m_split, p.times(8, 2 * g + 1))
                hi = mpl[:, :, MROW::32]
                lo = mpl[:, :, MROW + 1::32]
                src = negm[:].rearrange("p h t -> p t h")
                if k == 0:
                    nc.vector.tensor_copy(hi, src).then_inc(m_split, 1)
                else:
                    nc.vector.tensor_tensor(lo, src, hi, ALU.subtract).then_inc(m_split, 1)

            def add_m(p, g):
                dve.wait_ge(m_turned, p.times(4, g + 1))
                if p.after(16, 4 * (g - 1)):
                    dve.wait_ge(scoredT, p.times(16, 4 * (g - 1)))
                nc.vector.tensor_tensor(qM[:, g % 2, :], st_bank[0][:, 0:T],
                                        qS[:, g, :].bitcast(F32), ALU.add).then_inc(m_added, 1)

            def normalise(p, g, k):
                blocks = oT[:].rearrange("p (b r) -> p b r", r=32)
                if k == 0:
                    dve.wait_ge(pv_done, p.times(4, g - 1))
                    nc.vector.transpose(oT[:], pv_bank[:, (g % 2) * T:(g % 2) * T + T]).then_inc(turned_out, 1)
                elif k == 1:
                    dve.wait_ge(turned_out, p.times(4, g - 1))
                    nc.vector.reciprocal(rden[:], blocks[:, :, KCH:KCH + 1]).then_inc(inverted, 1)
                elif k == 2:
                    dve.wait_ge(inverted, p.times(4, g - 1))
                    nc.vector.tensor_tensor(blocks[:, :, 0:KCH], blocks[:, :, 0:KCH],
                                            rden[:].to_broadcast([P, T // 32, KCH]), ALU.mult).then_inc(divided, 1)
                else:
                    dve.wait_ge(divided, p.times(4, g - 1))
                    if p.after(1, -1):
                        dve.wait_ge(o_done, p.times(1, -1))
                    nc.vector.transpose(att[:, (g - 2) % GPP, :], oT[:]).then_inc(normed, 1)

            def glu_a(p, e):
                dve.wait_ge(tanh_done, p.times(8, e + 1))
                nc.vector.scalar_tensor_tensor(ug[:, e % 2, :], th[:, e % 2, :], 1.0, up_bank[e % 2][:, E:E + HID],
                                               ALU.add, ALU.mult).then_inc(u_done, 1)

            def glu_b(p, e):
                dve.wait_ge(u_done, p.times(8, e + 1))
                if e == 0:
                    dve.wait_ge(routed, p.times(ROUTES, ROUTES))
                    if p.after(3, 0):
                        dve.wait_ge(h_turned, p.times(3, 0))
                nc.vector.scalar_tensor_tensor(hid[:, e * HID:(e + 1) * HID], ug[:, e % 2, :], wts[:, e:e + 1],
                                               up_bank[e % 2][:, E + HID:E + UP], ALU.mult,
                                               ALU.mult).then_inc(h_done, 1)

            def glu(p, e):
                glu_a(p, e)
                glu_b(p, e)

            def split_h(p, r):
                dve.wait_ge(h_copied, p.times(3, r + 1))
                n = min(4, FCH - 4 * r)
                nc.vector.tensor_tensor(hT_lo[:, 4 * r:4 * r + n, :],
                                        turned_bank[r][:, 0:n * P].rearrange("p (k t) -> p k t", k=n),
                                        hT_hi[:, 4 * r:4 * r + n, :].bitcast(F32), ALU.subtract).then_inc(h_split, 1)

            def split_x2(p):
                dve.wait_ge(x2_copied, p.times(1, 1))
                nc.vector.tensor_tensor(xT2_lo[:], up_bank[0][:, 0:2 * P].rearrange("p (k t) -> p k t", k=2),
                                        xT2_hi[:].bitcast(F32), ALU.subtract).then_inc(x2_split, 1)

            def add_y(p, par):
                dve.wait_ge(y_done, p.times(1, 1))
                nc.vector.tensor_tensor(x1[:, par, :], up_bank[1][:, 0:T], x1[:, par, :], ALU.add).then_inc(y_added, 1)

            def residual_sum(p, par):
                dve.wait_ge(o_done, p.times(1, 1))
                dve.wait_ge(xres_done, p.times(1, 1))
                if p.known and p.v >= 2:
                    dve.wait_ge(stored[par], (p - 2).times(8, 16 - 8 * par))
                nc.vector.scalar_tensor_tensor(x1[:, par, :], up_bank[0][:, 0:T], tg[:, 0:1], xres[:, par, :],
                                               ALU.mult, ALU.add).then_inc(x1_done, 1)

            def best(p, k):
                if k == 0:
                    dve.wait_ge(sc_copied, p.times(1, 1))
                    if p.after(ROUTES, 0):
                        dve.wait_ge(routed, p.times(ROUTES, 0))
                    settled(dve)
                    nc.vector.max(top8[:], sc8[:]).then_inc(top2, 1)
                else:
                    dve.wait_ge(top2, p.times(2, 1))
                    settled(dve)
                    nc.vector.max_index(idx8[:], top8[:], sc8[:]).then_inc(top2, 1)

            def body(p, par):
                for g in range(GPP):
                    for h in range(GH):
                        if norm_here(p, g) and h < 2:
                            normalise(p, g, 2 * h)
                        if scores_here(p):
                            row_max(p, g, h)
                        if prev_here(p) and (g, h) == (2, 1):
                            split_x2(p - 1)
                        if norm_here(p, g) and h < 2:
                            normalise(p, g, 2 * h + 1)
                        if prev_here(p) and (g, h) == (2, 0):
                            norm_x1(p - 1, 1 - par, 2)
                        if next_here(p) and h == 0:
                            if g == 1 or g == 2:
                                rope(p + 1, g - 1)
                        if next_here(p) and g == 0 and h < 2:
                            norm_x(p + 1, 1 - par, h)
                        if prev2_here(p) and g == 0 and h < 3:
                            glu(p - 2, 4 + h)
                        if prev2_here(p) and (g, h) in ((1, 1), (1, 2)):
                            split_h(p - 2, h)
                        if prev2_here(p) and (g, h) == (2, 1):
                            add_y(p - 2, par)
                        if next_here(p) and (g, h) == (3, 0):
                            copy_v(p + 1, 1 - par)
                        if prev_here(p) and g == 3:
                            if h == 0:
                                glu_b(p - 1, 0)
                                glu_a(p - 1, 1)
                            elif h == 1:
                                glu_b(p - 1, 1)
                            elif h == 2:
                                glu(p - 1, 2)
                        if p.known and p.v == 0 and 5 <= 4 * g + h < 5 + SPLITS:
                            n = 4 * g + h - 5
                            dve.wait_ge(w_rounded, n + 1)
                            nc.vector.tensor_tensor(piece((wup_lo[:], wdn_lo[:]), n), staged(n),
                                                    piece((wup_hi[:].bitcast(F32), wdn_hi[:].bitcast(F32)), n),
                                                    ALU.subtract).then_inc(w_split, 1)
                    if scores_here(p):
                        split_m(p, g, 0)
                    if prev_here(p) and g == 1:
                        residual_sum(p - 1, 1 - par)
                    if prev_here(p) and g == 2:
                        best(p - 1, 0)
                    if scores_here(p):
                        split_m(p, g, 1)
                    if prev_here(p) and g == 1:
                        norm_x1(p - 1, 1 - par, 0)
                    if prev_here(p) and g == 2:
                        best(p - 1, 1)
                        glu_a(p - 1, 0)
                    if prev_here(p) and g == 3:
                        glu_a(p - 1, 3)
                    if scores_here(p):
                        add_m(p, g)
                    if prev2_here(p) and g == 0:
                        glu_a(p - 2, 7)
                        split_h(p - 2, 0)
                        glu_b(p - 2, 7)
                    if prev_here(p) and g == 1:
                        norm_x1(p - 1, 1 - par, 1)
                    if prev_here(p) and g == 3:
                        glu_b(p - 1, 3)

            nc.vector.memset(wp[:], 0.0).then_inc(zeroed, 1)
            nc.vector.memset(wo[:], 0.0).then_inc(zeroed, 1)
            nc.vector.memset(mpl[:], 0.0)
            nc.vector.memset(kM[:, 0:2].bitcast(F32), 0.0).then_inc(zeroed, 1)
            for k in range(2):
                norm_x(Pair(0), 0, k)
            dve.wait_ge(proj_in, 16 * 3)
            dve.wait_ge(tables_in, 16)
            rope(Pair(0), 0)
            rope(Pair(0), 1)
            dve.wait_ge(small_in, 16 * SMALL_DMAS)
            dve.wait_ge(pool_consts, 2)
            copy_v(Pair(0), 0)
            dve.wait_ge(consts_in, 16)
            nc.vector.tensor_copy(sel_r[:], cst[:, C_SEL:C_SEL + 16 * P].rearrange("p (a b c) -> p a b c", a=4, b=GPP))
            nc.vector.tensor_copy(ident_b[:], ident).then_inc(consts_r, 1)
            dve.wait_ge(tanh_g, 1)
            nc.vector.tensor_scalar(tgo[:], vec[:, 4:5], tg[:, 0:1], None, ALU.mult)
            nc.vector.tensor_scalar(tgh[:], tg[:, 1:2], 0.5, None, ALU.mult).then_inc(gates_ready, 1)
            bodies(dve, body)

        @block.gpsimd
        def _(pool):
            def split_qk(p, par, n):
                s = q_split if n == 0 else k_split
                pool.wait_ge(q_roped if n == 0 else k_roped, p.times(1, 1))
                nc.gpsimd.tensor_tensor(roped[:, n, :], rot_a[:, n, :], rot_b[:, n, :], ALU.add).then_inc(s, 1)
                pool.wait_ge(s, p.times(3, 1))
                if p.after(4, -4):
                    pool.wait_ge(stacked, p.times(4, -4))
                settled(pool)
                nc.gpsimd.tensor_copy(qk_hi[:, par, n, :], roped[:, n, :]).then_inc(s, 1)
                pool.wait_ge(s, p.times(3, 2))
                nc.gpsimd.tensor_tensor(qk_lo[:, par, n, :], roped[:, n, :], qk_hi[:, par, n, :].bitcast(F32),
                                        ALU.subtract).then_inc(s, 1)

            def residual(p, par):
                pool.wait_ge(x_in[par], p.times(16, 32 - 16 * par))
                if p.after(1, -1):
                    pool.wait_ge(x1_done, p.times(1, -1))
                settled(pool)
                nc.gpsimd.tensor_scalar(xres[:, par, :], xt[:, par, :], tgo[:, 0:1], None,
                                        ALU.add).then_inc(xres_done, 1)

            def inverse_root(p, s, steps, done, per, agg, shifted, inv):
                pool.wait_ge(s, p.times(steps, 2))
                settled(pool)
                nc.gpsimd.tensor_scalar(shifted[:], agg[:, 1:2], EPS, None, ALU.add).then_inc(done, 1)
                pool.wait_ge(done, p.times(per, 1))
                nc.gpsimd.tensor_tensor(inv[:], shifted[:], powers[:, 0:1], ALU.pow).then_inc(done, 1)

            def root_x(p):
                if p.after(1, 0):
                    pool.wait_ge(x_normed, p.times(1, 0))
                inverse_root(p, ln1, 2, root1, 3, mv, veps, rstd)
                pool.wait_ge(root1, p.times(3, 2))
                settled(pool)
                nc.gpsimd.tensor_scalar(shift[:], mv[:, 0:1], rstd[:, 0:1], -1.0, ALU.mult, ALU.mult).then_inc(root1, 1)

            def root_x1(p):
                inverse_root(p, ln2, 3, root2, 2, mv2, veps2, rstd2)

            def route(p):
                pool.wait_ge(top2, p.times(2, 2))
                settled(pool)
                nc.gpsimd.tensor_copy(idxf[:], idx8[:, 0:2]).then_inc(routed, 1)
                pool.wait_ge(dexp_done, p.times(1, 1))
                settled(pool)
                nc.gpsimd.tensor_scalar(rt[:, 1:2], rt[:, 0:1], 1.0, None, ALU.add).then_inc(routed, 1)
                pool.wait_ge(routed, p.times(ROUTES, 1))
                settled(pool)
                nc.gpsimd.tensor_scalar(oh[:, 1, :], iota8, idxf[:, 1:2], rt[:, 0:1], ALU.is_equal,
                                        ALU.mult).then_inc(routed, 1)
                pool.wait_ge(routed, p.times(ROUTES, 2))
                nc.gpsimd.tensor_tensor(rt[:, 2:3], rt[:, 1:2], powers[:, 1:2], ALU.pow).then_inc(routed, 1)
                nc.gpsimd.tensor_scalar(oh[:, 0, :], iota8, idxf[:, 0:1], None, ALU.is_equal).then_inc(routed, 1)
                pool.wait_ge(routed, p.times(ROUTES, 5))
                nc.gpsimd.tensor_tensor(oh[:, 0, :], oh[:, 0, :], oh[:, 1, :], ALU.add).then_inc(routed, 1)
                pool.wait_ge(routed, p.times(ROUTES, 6))
                if p.after(8, 0):
                    pool.wait_ge(h_done, p.times(8, 0))
                settled(pool)
                nc.gpsimd.tensor_scalar(wts[:], oh[:, 0, :], rt[:, 2:3], tgh[:, 0:1], ALU.mult,
                                        ALU.mult).then_inc(routed, 1)

            def body(p, par):
                if next_here(p):
                    root_x(p + 1)
                    split_qk(p + 1, 1 - par, 0)
                if prev_here(p):
                    root_x1(p - 1)
                if next_here(p):
                    split_qk(p + 1, 1 - par, 1)
                if prev_here(p):
                    route(p - 1)
                if next_here(p):
                    residual(p + 1, 1 - par)

            nc.gpsimd.memset(powers[:, 0:1], -0.5)
            nc.gpsimd.memset(powers[:, 1:2], -1.0).then_inc(pool_consts, 1)
            nc.gpsimd.memset(vE[:], 1.0).then_inc(pool_consts, 1)
            pool.wait_ge(pool_consts, 1)
            root_x(Pair(0))
            nc.gpsimd.memset(kM[:, 2:4].bitcast(F32), 0.0).then_inc(zeroed, 1)
            split_qk(Pair(0), 0, 0)
            split_qk(Pair(0), 0, 1)
            pool.wait_ge(gates_ready, 1)
            residual(Pair(0), 0)
            bodies(pool, body)


_OUTS = [((B, C, T), "float32")]


def kernel(**inputs):
    import numpy as _np
    import concourse.bacc as _bacc
    from concourse import mybir as _mybir
    from concourse.bass_utils import run_bass_kernel_spmd as _run

    a = {k: _np.asarray(v) for k, v in inputs.items()}
    turn = _np.arange(C).reshape(HEADS, 2, KCH // 2)[:, ::-1, :].reshape(C)
    wq, wk, wv = (a["L0_xattn_W" + n] for n in "qkv")
    bq, bk, bo = (a["L0_xattn_b" + n] for n in "qko")
    w_proj = _np.concatenate([wq.T, wq[turn].T, wk.T, wk[turn].T, wv.T], axis=1)
    vecs = _np.stack([_np.concatenate([v, v]) for v in (bq, bq[turn], bk, bk[turn], bo)], axis=1)
    bv = _np.concatenate([a["L0_xattn_bv"]] * (2 * TC))[None, :]
    gates = _np.concatenate([a["g_xattn"], a["g_ffn"]])[None, :]
    up = _np.concatenate([a["L0_ffn_W1"], a["L0_ffn_W2"]], axis=1).reshape(E * UP, T)
    w_up = _np.concatenate([a["L0_ffn_Wg"], up], axis=0).T
    w_down = a["L0_ffn_W3"].transpose(0, 2, 1).reshape(FCH, P, T).transpose(1, 0, 2)
    given = {"x": a["x"], "ctx": a["ctx_2048"], "w_proj": w_proj, "w_o": a["L0_xattn_Wo"].T, "vecs": vecs, "bv": bv,
             "gates": gates, "w_up": w_up, "w_down": w_down, "const": constants()}

    nc = _bacc.Bacc("TRN2", target_bir_lowering=False, num_devices=1)
    arrays, args = {}, []
    for name, v in given.items():
        v = _np.ascontiguousarray(v)
        arrays[f"in_{name}_dram"] = v
        args.append(nc.dram_tensor(f"in_{name}_dram", v.shape, _mybir.dt.from_np(v.dtype), kind="ExternalInput").ap())
    for i, (shape, dtype) in enumerate(_OUTS):
        dt = _mybir.dt.from_np(_np.dtype(dtype))
        args.append(nc.dram_tensor(f"out_{i}_dram", shape, dt, kind="ExternalOutput").ap())
    build(nc, *args)
    r = _run(nc, [arrays], core_ids=[0])
    return r.results[0]["out_0_dram"]
```

```python
from contextlib import ExitStack

import numpy as np

import concourse.bass as bass
from concourse import mybir

F32 = mybir.dt.float32
F32R = mybir.dt.float32r
BF16 = mybir.dt.bfloat16
U32 = mybir.dt.uint32
ALU = mybir.AluOpType
ACT = mybir.ActivationFunctionType
AX = mybir.AxisListType

B, C, T = 32, 64, 256
HEADS, KCH = 8, 8
E, HID = 8, 176
P = 128
PAIRS = B // 2
GH = 4
GPP = 2 * HEADS // GH
TC = T // P
SCALE = float(KCH) ** -0.5
EPS = 1e-5
FCH = E * HID // P
UP = 2 * HID
ROPES = 5
UGS = 4
ROUTES = 3
SPLITS = 6
SPLIT_STEPS = (0, 1, 2, 3, 4, 7)
UP_SPLITS = 4
PIECE = (E + E * UP) // 2
MROW = 3 * KCH

C_COS, C_SIN, C_ID, C_ONE, C_IOTA, C_SEL = 0, T, 2 * T, 2 * T + P, 2 * T + P + 1, 2 * T + P + 1 + E
C_ALL = C_SEL + 4 * P


def constants():
    inv = np.float32(1.0) / np.power(np.float32(10000.0), np.arange(0, KCH, 2, dtype=np.float32) / np.float32(KCH))
    f = np.arange(T, dtype=np.float32)[:, None] * inv.astype(np.float32)[None, :]
    f = np.concatenate([f, f], axis=-1)
    sign = np.where(np.arange(KCH) < KCH // 2, -1.0, 1.0).astype(np.float32)
    out = np.zeros((P, C_ALL), np.float32)
    out[:, C_COS:C_COS + T] = np.tile(np.cos(f).T, (P // KCH, 1))
    out[:, C_SIN:C_SIN + T] = np.tile((np.sin(f) * sign).T, (P // KCH, 1))
    rows = ((0, 1), (2,), (0, 2), (1,))
    sel = np.zeros((GPP, GH, KCH, 4, P), np.float32)
    for kind in range(4):
        for j in range(GH):
            for r in rows[kind]:
                for c in range(KCH):
                    sel[:, j, c, kind, 32 * j + r * KCH + c] = 1.0
    out[:, C_SEL:C_ALL] = sel.reshape(P, 4 * P)
    out[:, C_ID:C_ID + P] = np.eye(P, dtype=np.float32)
    for j in range(GH):
        out[32 * j + MROW:32 * j + MROW + 2, C_ONE] = 1.0
    out[:, C_IOTA:C_IOTA + E] = np.arange(E, dtype=np.float32)
    return out


class Pair:

    def __init__(self, v, least=None):
        self.v, self.least, self.known = v, least, least is None

    def __add__(self, n):
        return Pair(self.v + n, None if self.known else self.least + n)

    def __sub__(self, n):
        return Pair(self.v - n, None if self.known else self.least - n)

    def times(self, per, plus):
        assert (per * self.v if self.known else per * self.least) + plus > 0
        return self.v * per + plus if plus else self.v * per

    def after(self, per, plus):
        if self.known:
            return per * self.v + plus > 0
        assert per * self.least + plus > 0
        return True


def build(nc, x, ctx_in, w_proj, w_o, vecs, gates, w_up, w_down, const, out):
    x_d = x.rearrange("(n b) c t -> n (b c) t", b=2)
    c_d = ctx_in.rearrange("(n b) c t -> n (b c) t", b=2)
    o_d = out.rearrange("(n b) c t -> n (b c) t", b=2)

    with ExitStack() as stack:
        def sb(name, shape, dt=F32):
            return stack.enter_context(nc.sbuf_tensor(name, shape, dt))

        def bank(name):
            return stack.enter_context(nc.psum_tensor(name, [P, 512], F32))

        def sem(name):
            return stack.enter_context(nc.semaphore(name))

        cst = sb("cst", [P, C_ALL])
        cosT, sinT = cst[:, C_COS:C_COS + T], cst[:, C_SIN:C_SIN + T]
        ident = cst[:, C_ID:C_ID + P]
        m_rows_one = cst[:, C_ONE:C_ONE + 1]
        iota8 = cst[:, C_IOTA:C_IOTA + E]
        sel_r = sb("sel_r", [P, 4, GPP, P], F32R)
        ident_b = sb("ident_b", [P, P], BF16)
        wp = sb("wp", [P, 3, P])
        wo = sb("wo", [P, 2, C + 1])
        vec = sb("vec", [P, 3])
        gts = sb("gts", [P, 2])
        tg = sb("tg", [P, 2])
        tgo = sb("tgo", [P, 1])
        tgh = sb("tgh", [P, 1])
        w_stage = sb("w_stage", [P, 2, PIECE])
        wup_lo = sb("wup_lo", [P, 2, E + E * UP], F32R)
        wdn_lo = sb("wdn_lo", [P, FCH, T], F32R)
        wup_hi = sb("wup_hi", [P, 2, E + E * UP], F32R)
        wdn_hi = sb("wdn_hi", [P, FCH, T], F32R)
        xt = sb("xt", [P, 2, T])
        ct = sb("ct", [P, 2, T])
        stats = sb("stats", [P, 6])
        mv = sb("mv", [P, 2])
        rstd = sb("rstd", [P, 1])
        shift = sb("shift", [P, 1])
        xn = sb("xn", [P, T])
        qk = sb("qk", [P, 2, T])
        rotated = sb("rotated", [P, 2, T])
        rot_a = sb("rot_a", [P, 2, T])
        rot_b = sb("rot_b", [P, 2, T])
        roped = sb("roped", [P, 2, T])
        qk_hi = sb("qk_hi", [P, 2, 2, T], F32R)
        qk_lo = sb("qk_lo", [P, 2, 2, T], F32R)
        vE = sb("vE", [P, 2, TC, 2 * HEADS, 32])
        xres = sb("xres", [P, 2, T])
        qS = sb("qS", [P, GPP, T], F32R)
        kM = sb("kM", [P, GPP, GH, T], F32R)
        qM = sb("qM", [P, 2, T], F32R)
        negm = sb("negm", [P, GH, TC])
        mpl = sb("mpl", [P, TC, P], BF16)
        probs = sb("probs", [P, 2, GH, TC, T])
        powers = sb("powers", [P, 2])
        table_loaded = sb("table_loaded", [P, 2])
        veps, veps2 = sb("veps", [P, 1]), sb("veps2", [P, 1])
        oT = sb("oT", [P, 2, T])
        rden = sb("rden", [P, T // 32, 1])
        att = sb("att", [P, GPP, T])
        x1 = sb("x1", [P, 2, T])
        stats2 = sb("stats2", [P, 6])
        mv2 = sb("mv2", [P, 2])
        rstd2 = sb("rstd2", [P, 1])
        xn2 = sb("xn2", [P, T])
        xT2_hi = sb("xT2_hi", [P, 2, P], F32R)
        xT2_lo = sb("xT2_lo", [P, 2, P], F32R)
        sc8 = sb("sc8", [P, E])
        top8 = sb("top8", [P, 8])
        idx8 = sb("idx8", [P, 8], U32)
        idxf = sb("idxf", [P, 2])
        rt = sb("rt", [P, 8])
        oh = sb("oh", [P, 2, E])
        wts = sb("wts", [P, E])
        th = sb("th", [P, 2, HID])
        ug = sb("ug", [P, UGS, HID])
        hid = sb("hid", [P, E * HID])
        hT = sb("hT", [P, FCH, P])
        hT_hi = sb("hT_hi", [P, FCH, P], F32R)
        hT_lo = sb("hT_lo", [P, FCH, P], F32R)

        s_bank = [bank("s_bank0"), bank("s_bank1")]
        st_bank = [bank("st_bank0"), bank("st_bank1")]
        pv_bank = bank("pv_bank")
        up_bank = [bank("up_bank0"), bank("up_bank1")]
        misc = bank("misc")

        last_banks = (up_bank[0], s_bank[0], s_bank[1], misc, st_bank[0], st_bank[1], pv_bank, up_bank[1])

        def is_last(p):
            return p.known and p.v == PAIRS - 1

        def bank_of(p, e):
            if is_last(p):
                return last_banks[e]
            return up_bank[e % 2] if e < E - 1 else misc

        def turned_in(p, r):
            if is_last(p):
                return (s_bank[1], misc, st_bank[0])[r]
            return up_bank[(r + 1) % 2]

        def o_bank(p):
            return s_bank[0] if is_last(p) else up_bank[0]

        def y_bank(p):
            return s_bank[0] if is_last(p) else up_bank[1]

        proj_in, tables_in, consts_in = sem("proj_in"), sem("tables_in"), sem("consts_in")
        small_in, experts_in = sem("small_in"), [sem("experts_in0"), sem("experts_in1")]
        x_in = [sem("x_in0"), sem("x_in1")]
        stored = [sem("stored0"), sem("stored1")]
        x1_free = sem("x1_free")
        zeroed = sem("zeroed")
        waits_over = sem("waits_over")
        sel_zeroed = sem("sel_zeroed")
        tanh_g = sem("tanh_g")
        bv_projected = sem("bv_projected")
        gates_ready = sem("gates_ready")
        consts_r = sem("consts_r")
        q_proj, k_proj, v_proj = sem("q_proj"), sem("k_proj"), sem("v_proj")
        stacked, scored, scoredT = sem("stacked"), sem("scored"), sem("scoredT")
        m_turned, pv_done, o_done = sem("m_turned"), sem("pv_done"), sem("o_done")
        x2_turned, up_done, h_turned, y_done = sem("x2_turned"), sem("up_done"), sem("h_turned"), sem("y_done")
        stack_copied, exp_done = sem("stack_copied"), sem("exp_done")
        x_normed, q_copied, k_copied, v_copied = sem("x_normed"), sem("q_copied"), sem("k_copied"), sem("v_copied")
        x2_copied, sc_copied, tanh_done = sem("x2_copied"), sem("sc_copied"), sem("tanh_done")
        h_copied, dexp_done, w_rounded = sem("h_copied"), sem("dexp_done"), sem("w_rounded")
        ln1, ln2 = sem("ln1"), sem("ln2")
        q_rotated, k_rotated = sem("q_rotated"), sem("k_rotated")
        reduced, m_split, m_added = sem("reduced"), sem("m_split"), sem("m_added")
        turned_out, inverted, divided, normed, x1_done = sem("turned_out"), sem("inverted"), sem("divided"), sem("normed"), sem("x1_done")
        x2_split = sem("x2_split")
        top2, weighted, u_done, h_done, y_added = sem("top2"), sem("weighted"), sem("u_done"), sem("h_done"), sem("y_added")
        h_split, w_split = sem("h_split"), sem("w_split")
        root1, root2, pool_consts = sem("root1"), sem("root2"), sem("pool_consts")
        q_split, k_split, xres_done, routed = sem("q_split"), sem("k_split"), sem("xres_done"), sem("routed")

        SMALL_DMAS = 2

        LOOP_FROM = 2
        LOOP_TO = PAIRS - 2

        def settled(eng):
            eng.sem_inc(waits_over, 1)

        def bodies(eng, body):
            body(Pair(0), 0)
            body(Pair(1), 1)
            with eng.Fori(LOOP_FROM // 2, LOOP_TO // 2) as i:
                body(Pair(i * 2, LOOP_FROM), 0)
                body(Pair(i * 2 + 1, LOOP_FROM + 1), 1)
            for p in range(LOOP_TO, PAIRS + 2):
                body(Pair(p), p % 2)

        def at(p, low, high):
            if p.known:
                return low <= p.v <= high
            assert low <= LOOP_FROM and high >= LOOP_TO - 1
            return True

        def piece(tile, n):
            if n < UP_SPLITS:
                return tile[0][:, n // 2, (n % 2) * PIECE:(n % 2 + 1) * PIECE]
            return tile[1].rearrange("p k n -> p (k n)")[:, (n - UP_SPLITS) * FCH * T // 2:(n - UP_SPLITS + 1) * FCH * T // 2]

        def staged(n):
            return w_stage[:, n % 2, 0:PIECE if n < UP_SPLITS else FCH * T // 2]

        def scores_here(p):
            return at(p, 0, PAIRS - 1)

        def before_here(p, g):
            return at(p, 0 if g else 1, PAIRS if g == 0 else PAIRS - 1)

        def norm_here(p, g):
            return at(p, 0 if g > 1 else 1, PAIRS if g < 2 else PAIRS - 1)

        def next_here(p):
            return at(p, 0, PAIRS - 2)

        def next2_here(p):
            return at(p, 0, PAIRS - 3)

        def prev_here(p):
            return at(p, 1, PAIRS)

        def prev2_here(p):
            return at(p, 2, PAIRS + 1)

        block = stack.enter_context(nc.Block())

        @block.sync
        def _(sp):
            def load(p, par):
                if p.after(1, -1):
                    sp.wait_ge(xres_done, p.times(1, -1))
                    settled(sp)
                if p.after(1, -1):
                    sp.wait_ge(x_normed, p.times(1, -1))
                    settled(sp)
                if p.after(1, -1):
                    sp.wait_ge(v_proj, p.times(1, -1))
                    settled(sp)
                sp.dma_start(xt[:, par, :], x_d[p.v, :, :]).then_inc(x_in[par], 16)
                sp.dma_start(ct[:, par, :], c_d[p.v, :, :]).then_inc(x_in[par], 16)

            load(Pair(0), 0)
            sp.dma_start(wp[:], w_proj).then_inc(proj_in, 16)
            sp.dma_start(vec[:], vecs).then_inc(proj_in, 16)
            sp.dma_start(cst[:, 0:C_SEL], const[:, 0:C_SEL]).then_inc(tables_in, 16)
            sp.dma_start(cst[:, C_SEL:C_ALL], const[:, C_SEL:C_ALL]).then_inc(consts_in, 16)
            sp.dma_start(gts[:], gates.to_broadcast([P, 2])).then_inc(small_in, 16)
            sp.dma_start(wo[:], w_o).then_inc(small_in, 16)
            load(Pair(1), 1)
            w_d = (w_up.rearrange("(k p) n -> p k n", p=P), w_down)
            def load_piece(n):
                sp.dma_start(staged(n), piece(w_d, n)).then_inc(experts_in[n % 2], 16)

            load_piece(0)
            load_piece(1)

            def body(p, par):
                if next2_here(p):
                    load(p + 2, par)
                if p.known and p.v == 0:
                    for n in range(2, SPLITS):
                        sp.wait_ge(w_split, n - 1)
                        load_piece(n)
                if prev2_here(p):
                    sp.wait_ge(y_added, p.times(1, -1))
                    settled(sp)
                    sp.dma_start(o_d[(p - 2).v, :, :], x1[:, par, :]).then_inc(stored[par], 16)
                    sp.wait_ge(stored[par], (p - 2).times(8, 16 - 8 * par))
                sp.sem_inc(x1_free, 1)

            bodies(sp, body)
            sp.wait_ge(stored[0], 16 * (PAIRS // 2))
            sp.wait_ge(stored[1], 16 * (PAIRS // 2))

        @block.tensor
        def _(pe):
            def score(p, g, h):
                G4 = 4 * g + h
                if h == 0:
                    pe.wait_ge(stack_copied, p.times(4, g + 1))
                if p.after(16, G4 - 1):
                    pe.wait_ge(reduced, p.times(16, G4 - 1))
                for t in range(TC):
                    mm = pe.matmul(s_bank[h % 2][:, t * T:(t + 1) * T], qS[:, g, t * P:(t + 1) * P],
                                   kM[:, g, h, :], start=True, stop=True)
                mm.then_inc(scored, 1)

            def score_t(p, g, h):
                n = 4 * (g - 1) + h
                if h == 0:
                    pe.wait_ge(m_added, p.times(4, g))
                if p.after(16, n - 1):
                    pe.wait_ge(exp_done, p.times(16, n - 1))
                for s in range(TC):
                    mm = pe.matmul(st_bank[h % 2][:, s * T:(s + 1) * T],
                                   kM[:, (g - 1) % GPP, h, s * P:(s + 1) * P], qM[:, (g - 1) % 2, :],
                                   start=True, stop=True)
                mm.then_inc(scoredT, 1)

            def weigh(p, g, s):
                par = (g - 1) % 2
                vpar = PARITY[0] if g else 1 - PARITY[0]
                gg = (g - 1) % GPP
                if s == 0:
                    pe.wait_ge(exp_done, p.times(16, 4 * g))
                    if p.after(4, g - 1):
                        pe.wait_ge(turned_out, p.times(4, g - 1))
                for j in range(GH):
                    mm = pe.matmul(pv_bank[32 * j:32 * j + 32, (gg % 2) * T:(gg % 2) * T + T],
                                   vE[:, vpar, s, gg * GH + j, :], probs[:, par, j, s, :],
                                   start=(s == 0), stop=(s == TC - 1))
                if s == TC - 1:
                    mm.then_inc(pv_done, 1)

            def turn_m(p, g):
                pe.wait_ge(m_split, p.times(8, 2 * g + 2))
                if p.after(16, 4 * g - 1):
                    pe.wait_ge(exp_done, p.times(16, 4 * g - 1))
                for t in range(TC):
                    mm = pe.matmul(st_bank[0][:, t * P:(t + 1) * P], mpl[:, t, :], ident_b[:],
                                   start=True, stop=True)
                mm.then_inc(m_turned, 1)

            def stack_qk(p, g, par):
                for n in range(2):
                    for part, src in enumerate((qk_hi, qk_lo)):
                        mm = pe.matmul(misc[:, n * T:(n + 1) * T], sel_r[:, 2 * n + part, g, :], src[:, par, n, :],
                                       start=(part == 0), stop=(part == 1))
                mm.then_inc(stacked, 1)

            def project(p, par, n, bank=misc):
                src = xn[:] if n == 0 else ct[:, par, :]
                if n == 0:
                    pe.wait_ge(x_normed, p.times(1, 1))
                else:
                    pe.wait_ge(x_in[par], p.times(16, 32 - 16 * par))
                pe.matmul(bank[:, 0:T], wp[:, n, :], src, start=True,
                          stop=True).then_inc(q_proj if n == 0 else k_proj, 1)

            def project_v(p, par, bank=misc):
                for s in range(TC):
                    mm = pe.matmul(bank[:, s * P:(s + 1) * P], ct[:, par, s * P:(s + 1) * P], wp[:, 2, :],
                                   start=True, stop=True)
                mm.then_inc(v_proj, 1)

            def project_o(p):
                pe.wait_ge(normed, p.times(4, 4))
                if p.after(3, -1) and not is_last(p):
                    pe.wait_ge(h_copied, p.times(3, -1))
                for g in range(2):
                    for b in range(2):
                        mm = pe.matmul(o_bank(p)[b * C:(b + 1) * C, 0:T], wo[:, g, 0:C], att[:, 2 * b + g, :],
                                       start=(g == 0), stop=(g == 1))
                mm.then_inc(o_done, 1)

            def turn_x2(p):
                pe.wait_ge(ln2, p.times(3, 3))
                for k in range(2):
                    mm = pe.transpose(up_bank[0][:, k * P:(k + 1) * P], xn2[:, k * P:(k + 1) * P], ident)
                mm.then_inc(x2_turned, 1)

            def up(p, e):
                if e == 0:
                    pe.wait_ge(x2_split, p.times(1, 1))
                    if p.known and p.v == 0:
                        pe.wait_ge(w_split, UP_SPLITS)
                if e == 1 and not is_last(p) and p.after(1, 0):
                    pe.wait_ge(y_added, p.times(1, 0))
                if 1 < e < E - 1 and not is_last(p):
                    pe.wait_ge(h_done, p.times(8, e - 1))
                if e == E - 1 and (not p.known or p.v + 3 < PAIRS):
                    pe.wait_ge(q_copied, p.times(1, 4))
                elif e == E - 1 and p.v + 2 < PAIRS:
                    pe.wait_ge(stack_copied, p.times(4, 10))
                if e == E - 1 and is_last(p):
                    pe.wait_ge(y_added, p.times(1, 0))
                cols = slice(0, E + UP) if e == 0 else slice(E + e * UP, E + (e + 1) * UP)
                at_ = 0 if e == 0 else E
                parts = ((xT2_hi, wup_hi[:]), (xT2_hi, wup_lo[:]), (xT2_lo, wup_hi[:]))
                for n, (a, w) in enumerate(parts):
                    for k in range(2):
                        mm = pe.matmul(bank_of(p, e)[:, at_:E + UP], a[:, k, :], w[:, k, cols],
                                       start=(n == 0 and k == 0), stop=(n == 2 and k == 1))
                mm.then_inc(up_done, 1)

            def turn_h(p, r):
                pe.wait_ge(h_done, p.times(8, (3, 6, 8)[r] if is_last(p) else 6 + r))
                if r == 2 and not is_last(p):
                    pe.wait_ge(h_copied, p.times(3, 1))
                for k in range(4 * r, min(4 * r + 4, FCH)):
                    mm = pe.transpose(turned_in(p, r)[:, (k % 4) * P:(k % 4 + 1) * P], hid[:, k * P:(k + 1) * P], ident)
                mm.then_inc(h_turned, 1)

            def down(p, low, high):
                if low == 0 and p.known and p.v == 0:
                    pe.wait_ge(w_split, SPLITS)
                if low == 0 and not is_last(p):
                    pe.wait_ge(h_copied, p.times(3, 3))
                pe.wait_ge(h_split, p.times(3, (high + 3) // 4))
                for k in range(low, high):
                    for n, (a, w) in enumerate(((hT_hi, wdn_hi[:]), (hT_hi, wdn_lo[:]), (hT_lo, wdn_hi[:]))):
                        mm = pe.matmul(y_bank(p)[:, 0:T], a[:, k, :], w[:, k, :],
                                       start=(k == 0 and n == 0), stop=(k == FCH - 1 and n == 2))
                if high == FCH:
                    mm.then_inc(y_done, 1)

            PARITY = [0]

            def stack_next(p, g, par):
                if g < 3:
                    if g == 1 and next_here(p):
                        pe.wait_ge(k_copied, p.times(1, 2))
                    elif g == 1:
                        pe.wait_ge(h_done, p.times(8, -8))
                    else:
                        pe.wait_ge(stack_copied, p.times(4, g + 1))
                    stack_qk(p, g + 1, par)
                elif next_here(p):
                    pe.wait_ge(q_split, p.times(ROPES, 2 * ROPES))
                    pe.wait_ge(k_split, p.times(ROPES, 2 * ROPES))
                    pe.wait_ge(v_copied, p.times(1, 2))
                    stack_qk(p + 1, 0, 1 - par)

            def body(p, par):
                PARITY[0] = par
                for g in range(GPP):
                    for h in range(GH):
                        if scores_here(p) and (g, h) == (2, 2):
                            stack_next(p, g, par)
                        if prev_here(p) and (g, h) == (2, 1):
                            turn_x2(p - 1)
                            if is_last(p - 1):
                                down(p - 2, 7, FCH)
                        if next_here(p) and (g, h) == (3, 0):
                            pe.wait_ge(stack_copied, p.times(4, 4))
                            project_v(p + 1, 1 - par)
                        if scores_here(p):
                            score(p, g, h)
                        if before_here(p, g):
                            score_t(p, g, h)
                        if scores_here(p) and (g, h) in ((0, 0), (1, 3), (3, 1)):
                            stack_next(p, g, par)
                        if prev2_here(p) and (g, h) == (1, 0) and is_last(p - 2):
                            turn_h(p - 2, 1)
                            down(p - 2, 0, 4)
                            turn_h(p - 2, 2)
                            down(p - 2, 4, 8)
                            down(p - 2, 8, FCH)
                        elif prev2_here(p) and (g, h) == (1, 0):
                            turn_h(p - 2, 1)
                            turn_h(p - 2, 2)
                        if next_here(p) and (g, h) == (0, 2):
                            pe.wait_ge(stack_copied, p.times(4, 2))
                            project(p + 1, 1 - par, 0)
                        if prev2_here(p) and (g, h) == (0, 2):
                            turn_h(p - 2, 0)
                        if next_here(p) and (g, h) == (1, 1):
                            if prev2_here(p):
                                pe.wait_ge(h_done, p.times(8, -8))
                            else:
                                pe.wait_ge(q_copied, p.times(1, 2))
                            project(p + 1, 1 - par, 1)
                        if prev2_here(p):
                            if g == 0 and h < 2:
                                up(p - 2, 5 + h)
                            if g == 0 and h == 3:
                                up(p - 2, 7)
                        if prev_here(p):
                            if g == 1 and h == 2:
                                project_o(p - 1)
                        if prev2_here(p) and not is_last(p - 2):
                            if g == 1 and h == 2:
                                down(p - 2, 0, 3)
                            if g == 1 and h == 3:
                                down(p - 2, 3, 7)
                            if g == 2 and h == 0 and not is_last(p - 1):
                                down(p - 2, 7, FCH)
                        if prev_here(p):
                            if g == 2 and h > 1:
                                up(p - 1, h - 2)
                            if g == 3 and h > 0:
                                up(p - 1, 1 + h)
                    turn_first = p.known and GPP * p.v + g < GPP + 2
                    if scores_here(p) and turn_first:
                        turn_m(p, g)
                    if before_here(p, g):
                        weigh(p, g, 0)
                    if scores_here(p) and not turn_first:
                        turn_m(p, g)
                    if before_here(p, g):
                        weigh(p, g, 1)

            pe.wait_ge(proj_in, 16 * 2)
            project(Pair(0), 0, 1, up_bank[0])
            project(Pair(0), 0, 0)
            project_v(Pair(0), 0, up_bank[1])
            pe.wait_ge(q_copied, 1)
            pe.wait_ge(consts_r, 2)
            pe.wait_ge(q_split, ROPES)
            pe.wait_ge(k_split, ROPES)
            stack_qk(Pair(0), 0, 0)
            pe.wait_ge(small_in, 16 * SMALL_DMAS)
            pe.wait_ge(k_copied, 1)
            for g in range(2):
                for b in range(2):
                    mm = pe.matmul(up_bank[0][b * C:(b + 1) * C, 0:1], wo[:, g, 0:C], wo[:, g, C:C + 1],
                                   start=(g == 0), stop=(g == 1))
            mm.then_inc(bv_projected, 1)
            bodies(pe, body)

        @block.scalar
        def _(act):
            def expo(p, g, h):
                n = 4 * (g - 1) + h
                act.wait_ge(scoredT, p.times(16, n + 1))
                if p.after(4, g - 2):
                    act.wait_ge(pv_done, p.times(4, g - 2))
                nc.scalar.activation(probs[:, (g - 1) % 2, h, :, :].rearrange("p s t -> p (s t)"), st_bank[h % 2][:],
                                     ACT.Exp, scale=SCALE).then_inc(exp_done, 1)

            def copy_stack(p, g, half):
                if half == 0:
                    act.wait_ge(stacked, p.times(4, g + 1))
                    if p.after(16, 4 * (g - 3)):
                        act.wait_ge(scoredT, p.times(16, 4 * (g - 3)))
                    nc.scalar.activation(qS[:, g, :], misc[:, 0:T], ACT.Identity)
                for j in range(2 * half, 2 * half + 2):
                    rows = slice(32 * j, 32 * j + 32)
                    last = nc.scalar.activation(kM[rows, g, j, :], misc[rows, T:2 * T], ACT.Identity,
                                                bias=m_rows_one[rows, :])
                if half == 1:
                    last.then_inc(stack_copied, 1)

            def copy_next(p, g, half):
                if g < 3:
                    copy_stack(p, g + 1, half)
                elif next_here(p):
                    copy_stack(p + 1, 0, half)

            def copy_h(p, r):
                act.wait_ge(h_turned, p.times(3, r + 1))
                n = min(4, FCH - 4 * r) * P
                for to in (hT_hi,) if is_last(p) else (hT_hi, hT):
                    last = nc.scalar.activation(to[:, 4 * r:4 * r + n // P, :].rearrange("p k t -> p (k t)"),
                                                turned_in(p, r)[:, 0:n], ACT.Identity)
                last.then_inc(h_copied, 1)

            def copy_qk(p, n, bank=misc):
                act.wait_ge(q_proj if n == 0 else k_proj, p.times(1, 1))
                if p.after(ROPES, 0):
                    act.wait_ge(q_split if n == 0 else k_split, p.times(ROPES, 0))
                nc.scalar.activation(qk[:, n, :], bank[:, 0:T], ACT.Identity,
                                     bias=vec[:, n:n + 1]).then_inc(q_copied if n == 0 else k_copied, 1)

            def copy_v(p, par, bank=misc):
                act.wait_ge(v_proj, p.times(1, 1))
                if p.after(4, -4):
                    act.wait_ge(pv_done, p.times(4, -4))
                nc.scalar.activation(vE[:, par, :, :, 0:KCH],
                                     bank[:, 0:T].rearrange("p (s h c) -> p s h c", s=TC, c=KCH),
                                     ACT.Identity).then_inc(v_copied, 1)

            def norm_x(p, par):
                act.wait_ge(root1, p.times(3, 3))
                if p.after(1, 0):
                    act.wait_ge(q_proj, p.times(1, 0))
                nc.scalar.activation(xn[:], xt[:, par, :], ACT.Identity, scale=rstd[:, 0:1],
                                     bias=shift[:, 0:1]).then_inc(x_normed, 1)

            def tanh(p, e):
                act.wait_ge(up_done, p.times(8, e + 1))
                if p.after(8, e - 1):
                    act.wait_ge(u_done, p.times(8, e - 1))
                nc.scalar.activation(th[:, e % 2, :], bank_of(p, e)[:, E:E + HID], ACT.Tanh,
                                     scale=0.5).then_inc(tanh_done, 1)

            def body(p, par):
                for g in range(GPP):
                    for h in range(GH):
                        if prev_here(p) and g == 3 and h == 0:
                            tanh(p - 1, 1)
                        if next_here(p) and (g, h) == (3, 0):
                            copy_v(p + 1, 1 - par)
                        if prev_here(p) and (g, h) == (2, 1):
                            act.wait_ge(x2_turned, p.times(1, 0))
                            if p.after(8, -8):
                                act.wait_ge(up_done, p.times(8, -8))
                            nc.scalar.activation(xT2_hi[:].rearrange("p k t -> p (k t)"), up_bank[0][:, 0:2 * P],
                                                 ACT.Identity).then_inc(x2_copied, 1)
                        if prev_here(p) and g == 2 and h == 3:
                            act.wait_ge(up_done, p.times(8, -7))
                            if p.after(3, -3):
                                act.wait_ge(top2, p.times(3, -3))
                            nc.scalar.activation(sc8[:], up_bank[0][:, 0:E], ACT.Identity).then_inc(sc_copied, 1)
                        if scores_here(p) and g > 1 and h == 2:
                            copy_next(p, g, 0)
                        if scores_here(p) and (g, h) == (0, 1):
                            copy_next(p, g, 1)
                        if before_here(p, g):
                            expo(p, g, h)
                        if prev_here(p) and (g, h) == (2, 3):
                            act.wait_ge(top2, p.times(3, -2))
                            if p.after(ROUTES, -ROUTES):
                                act.wait_ge(routed, p.times(ROUTES, -ROUTES))
                            nc.scalar.activation(rt[:, 0:1], top8[:, 0:1], ACT.Exp, scale=-1.0,
                                                 bias=top8[:, 1:2]).then_inc(dexp_done, 1)
                        if scores_here(p) and (g, h) == (1, 3):
                            copy_next(p, g, 0)
                        if scores_here(p) and g and h == 3:
                            copy_next(p, g, 1)
                        if scores_here(p) and (g, h) == (0, 0):
                            copy_next(p, g, 0)
                        if prev_here(p) and (g, h) == (2, 3):
                            tanh(p - 1, 0)
                        if prev2_here(p) and (g, h) == (0, 3):
                            if is_last(p - 2):
                                copy_h(p - 2, 0)
                            tanh(p - 2, 7)
                            if not is_last(p - 2):
                                copy_h(p - 2, 0)
                        if next_here(p) and (g, h) in ((0, 2), (1, 1)):
                            copy_qk(p + 1, g)
                        if next2_here(p) and (g, h) == (3, 1):
                            norm_x(p + 2, par)
                        if prev2_here(p):
                            if g == 0 and h < 2:
                                tanh(p - 2, 5 + h)
                            if g == 1 and h == 0:
                                copy_h(p - 2, 1)
                                copy_h(p - 2, 2)
                        if prev_here(p):
                            if g == 3 and h > 0:
                                tanh(p - 1, 1 + h)
                    step = GPP * p.v + g if p.known else None
                    if step in SPLIT_STEPS:
                        n = SPLIT_STEPS.index(step)
                        act.wait_ge(experts_in[n % 2], 16 * (n // 2 + 1))
                        nc.scalar.activation(piece((wup_hi[:], wdn_hi[:]), n), staged(n),
                                             ACT.Identity).then_inc(w_rounded, 1)

            act.wait_ge(pool_consts, 1)
            nc.scalar.activation(table_loaded[:], powers[:], ACT.Exp)
            act.wait_ge(proj_in, 16 * 2)
            copy_qk(Pair(0), 1, up_bank[0])
            norm_x(Pair(0), 0)
            act.wait_ge(consts_in, 16)
            act.wait_ge(sel_zeroed, 1)
            for g in range(GPP):
                if g == GPP // 2:
                    copy_qk(Pair(0), 0)
                rows = slice(g * GH * KCH, (g + 1) * GH * KCH)
                last = nc.scalar.activation(sel_r[rows, :, g, :], cst[rows, C_SEL:C_ALL].rearrange("p (a c) -> p a c", a=4),
                                            ACT.Identity)
            last.then_inc(consts_r, 1)
            act.wait_ge(pool_consts, 2)
            copy_v(Pair(0), 0, up_bank[1])
            act.wait_ge(tables_in, 16)
            act.wait_ge(zeroed, 2)
            copy_stack(Pair(0), 0, 0)
            copy_stack(Pair(0), 0, 1)
            act.wait_ge(small_in, 16 * SMALL_DMAS)
            nc.scalar.activation(tg[:], gts[:], ACT.Tanh).then_inc(tanh_g, 1)
            norm_x(Pair(1), 1)
            bodies(act, body)

        @block.vector
        def _(dve):
            def ln_step(s, rooted, k, steps, p, src, mid, agg, inv, dst):
                if k == 0:
                    nc.vector.bn_stats(mid[:], src).then_inc(s, 1)
                elif k == 1:
                    dve.wait_ge(s, p.times(steps, 1))
                    settled(dve)
                    nc.vector.bn_aggr(agg[:], mid[:]).then_inc(s, 1)
                else:
                    dve.wait_ge(rooted, p.times(2, 2))
                    nc.vector.tensor_scalar(dst[:], src, agg[:, 0:1], inv[:, 0:1], ALU.subtract,
                                            ALU.mult).then_inc(s, 1)

            def norm_x(p, par, k):
                if k == 0:
                    dve.wait_ge(x_in[par], p.times(16, 32 - 16 * par))
                ln_step(ln1, None, k, 2, p, xt[:, par, :], stats, mv, None, None)

            def norm_x1(p, par, k):
                if k == 0:
                    dve.wait_ge(x1_done, p.times(1, 1))
                if k == 2:
                    if p.after(1, 0):
                        dve.wait_ge(x2_turned, p.times(1, 0))
                ln_step(ln2, root2, k, 3, p, x1[:, par, :], stats2, mv2, rstd2, xn2)

            def rotate(p, n):
                dve.wait_ge(q_copied if n == 0 else k_copied, p.times(1, 1))
                if p.after(ROPES, 0):
                    dve.wait_ge(q_split if n == 0 else k_split, p.times(ROPES, 0))
                settled(dve)
                nc.vector.stream_shuffle(rotated[:, n, :], qk[:, n, :],
                                         [i ^ (KCH // 2) for i in range(32)]).then_inc(q_rotated if n == 0 else k_rotated, 1)

            def row_max(p, g, h):
                dve.wait_ge(scored, p.times(16, 4 * g + h + 1))
                nc.vector.tensor_reduce(negm[:, h, :], s_bank[h % 2][:].rearrange("p (t s) -> p t s", t=TC), AX.X,
                                        ALU.max, negate=True).then_inc(reduced, 1)

            def split_m(p, g, k):
                if k == 0:
                    dve.wait_ge(reduced, p.times(16, 4 * g + 4))
                    if p.after(4, g):
                        dve.wait_ge(m_turned, p.times(4, g))
                else:
                    dve.wait_ge(m_split, p.times(8, 2 * g + 1))
                hi = mpl[:, :, MROW::32]
                lo = mpl[:, :, MROW + 1::32]
                src = negm[:].rearrange("p h t -> p t h")
                if k == 0:
                    nc.vector.tensor_copy(hi, src).then_inc(m_split, 1)
                else:
                    nc.vector.tensor_tensor(lo, src, hi, ALU.subtract).then_inc(m_split, 1)

            def add_m(p, g):
                dve.wait_ge(m_turned, p.times(4, g + 1))
                if p.after(16, 4 * (g - 1)):
                    dve.wait_ge(scoredT, p.times(16, 4 * (g - 1)))
                nc.vector.tensor_tensor(qM[:, g % 2, :], st_bank[0][:, 0:T],
                                        qS[:, g, :].bitcast(F32), ALU.add).then_inc(m_added, 1)

            def normalise(p, g, k):
                blocks = oT[:, g % 2, :].rearrange("p (b r) -> p b r", r=32)
                if k == 0:
                    dve.wait_ge(pv_done, p.times(4, g - 1))
                    nc.vector.transpose(oT[:, g % 2, :], pv_bank[:, (g % 2) * T:(g % 2) * T + T]).then_inc(turned_out, 1)
                elif k == 1:
                    dve.wait_ge(turned_out, p.times(4, g - 1))
                    nc.vector.reciprocal(rden[:], blocks[:, :, KCH:KCH + 1]).then_inc(inverted, 1)
                elif k == 2:
                    dve.wait_ge(inverted, p.times(4, g - 1))
                    nc.vector.tensor_tensor(blocks[:, :, 0:KCH], blocks[:, :, 0:KCH],
                                            rden[:].to_broadcast([P, T // 32, KCH]), ALU.mult).then_inc(divided, 1)
                else:
                    dve.wait_ge(divided, p.times(4, g - 1))
                    if g < 3 and p.after(1, -1):
                        dve.wait_ge(o_done, p.times(1, -1))
                    nc.vector.transpose(att[:, (g - 2) % GPP, :], oT[:, g % 2, :]).then_inc(normed, 1)

            def glu_a(p, e):
                dve.wait_ge(tanh_done, p.times(8, e + 1))
                if is_last(p) and e >= UGS:
                    dve.wait_ge(h_done, p.times(8, e - UGS + 1))
                nc.vector.scalar_tensor_tensor(ug[:, e % UGS, :], th[:, e % 2, :], 1.0, bank_of(p, e)[:, E:E + HID],
                                               ALU.add, ALU.mult).then_inc(u_done, 1)

            def glu_b(p, e):
                dve.wait_ge(u_done, p.times(8, e + 1))
                if e == 0:
                    dve.wait_ge(weighted, p.times(2, 2))
                    if p.after(3, 0):
                        dve.wait_ge(h_turned, p.times(3, 0))
                nc.vector.scalar_tensor_tensor(hid[:, e * HID:(e + 1) * HID], ug[:, e % UGS, :], wts[:, e:e + 1],
                                               bank_of(p, e)[:, E + HID:E + UP], ALU.mult,
                                               ALU.mult).then_inc(h_done, 1)

            def glu(p, e):
                glu_a(p, e)
                glu_b(p, e)

            def glus_last(p):
                glu_b(p, 0)
                for e in range(1, E - UGS):
                    glu_b(p, e)
                    glu_a(p, e + UGS - 1)
                for e in range(E - UGS, E - 1):
                    glu_b(p, e)
                split_h(p, 0)
                glu_a(p, E - 1)
                glu_b(p, E - 1)
                split_h(p, 1)
                split_h(p, 2)

            def split_h(p, r):
                dve.wait_ge(h_copied, p.times(3, r + 1))
                n = min(4, FCH - 4 * r)
                nc.vector.tensor_tensor(hT_lo[:, 4 * r:4 * r + n, :],
                                        turned_in(p, r)[:, 0:n * P].rearrange("p (k t) -> p k t", k=n),
                                        hT_hi[:, 4 * r:4 * r + n, :].bitcast(F32), ALU.subtract).then_inc(h_split, 1)

            def split_x2(p):
                dve.wait_ge(x2_copied, p.times(1, 1))
                nc.vector.tensor_tensor(xT2_lo[:], up_bank[0][:, 0:2 * P].rearrange("p (k t) -> p k t", k=2),
                                        xT2_hi[:].bitcast(F32), ALU.subtract).then_inc(x2_split, 1)

            def add_y(p, par):
                dve.wait_ge(y_done, p.times(1, 1))
                nc.vector.tensor_tensor(x1[:, par, :], y_bank(p)[:, 0:T], x1[:, par, :], ALU.add).then_inc(y_added, 1)

            def residual_sum(p, par):
                dve.wait_ge(o_done, p.times(1, 1))
                dve.wait_ge(xres_done, p.times(1, 1))
                dve.wait_ge(x1_free, p.times(1, 1))
                nc.vector.scalar_tensor_tensor(x1[:, par, :], o_bank(p)[:, 0:T], tg[:, 0:1], xres[:, par, :],
                                               ALU.mult, ALU.add).then_inc(x1_done, 1)

            def best(p, k):
                if k == 0:
                    dve.wait_ge(sc_copied, p.times(1, 1))
                    if p.after(ROUTES, 0):
                        dve.wait_ge(routed, p.times(ROUTES, 0))
                    settled(dve)
                    nc.vector.max(top8[:], sc8[:]).then_inc(top2, 1)
                elif k == 1:
                    dve.wait_ge(top2, p.times(3, 1))
                    settled(dve)
                    nc.vector.max_index(idx8[:], top8[:], sc8[:]).then_inc(top2, 1)
                else:
                    dve.wait_ge(top2, p.times(3, 2))
                    settled(dve)
                    nc.vector.tensor_copy(idxf[:], idx8[:, 0:2]).then_inc(top2, 1)

            def weight(p, k):
                if k == 0:
                    dve.wait_ge(routed, p.times(ROUTES, ROUTES))
                    settled(dve)
                    nc.vector.scalar_tensor_tensor(oh[:, 0, :], iota8, idxf[:, 0:1], oh[:, 1, :],
                                                   ALU.is_equal, ALU.add).then_inc(weighted, 1)
                else:
                    dve.wait_ge(weighted, p.times(2, 1))
                    if p.after(8, 0):
                        dve.wait_ge(h_done, p.times(8, 0))
                    settled(dve)
                    nc.vector.tensor_scalar(wts[:], oh[:, 0, :], rt[:, 2:3], tgh[:, 0:1], ALU.mult,
                                            ALU.mult).then_inc(weighted, 1)

            def body(p, par):
                for g in range(GPP):
                    for h in range(GH):
                        if norm_here(p, g) and h < 2 and (g, h) != (1, 1):
                            normalise(p, g, 2 * h)
                        if prev2_here(p) and (g, h) == (0, 1) and not is_last(p - 2):
                            glu(p - 2, 5)
                        if prev_here(p) and (g, h) == (2, 1):
                            split_x2(p - 1)
                        if prev_here(p) and (g, h) == (3, 1) and not is_last(p - 1):
                            glu_b(p - 1, 1)
                        if prev_here(p) and (g, h) == (3, 2) and not is_last(p - 1):
                            glu(p - 1, 2)
                        if prev_here(p) and (g, h) == (3, 0):
                            weight(p - 1, 0)
                        if norm_here(p, g) and (g, h) == (3, 0):
                            normalise(p, g, 1)
                        if prev_here(p) and (g, h) == (3, 0):
                            weight(p - 1, 1)
                            if not is_last(p - 1):
                                glu_b(p - 1, 0)
                        if norm_here(p - 1, 3) and (g, h) == (0, 3):
                            normalise(p - 1, 3, 3)
                        if scores_here(p):
                            row_max(p, g, h)
                        if prev_here(p) and (g, h) == (2, 3):
                            best(p - 1, 0)
                        if prev2_here(p) and (g, h) == (0, 0):
                            if is_last(p - 2):
                                glus_last(p - 2)
                            else:
                                glu(p - 2, 4)
                        if norm_here(p, g) and (g, h) in ((0, 0), (1, 0), (2, 0)):
                            normalise(p, g, 2 * h + 1)
                        if norm_here(p, g) and (g, h) == (1, 0):
                            normalise(p, g, 2)
                            normalise(p, g, 3)
                        if next_here(p) and (g, h) == (1, 0):
                            rotate(p + 1, 0)
                        if prev_here(p) and (g, h) == (2, 0):
                            norm_x1(p - 1, 1 - par, 2)
                        if next_here(p):
                            if (g, h) == (1, 2):
                                rotate(p + 1, 1)
                        if next2_here(p) and (g, h) in ((1, 2), (2, 0)):
                            norm_x(p + 2, par, g - 1)
                        if prev2_here(p) and (g, h) == (2, 1) and not (p.known and p.v >= PAIRS):
                            add_y(p - 2, par)
                        if prev_here(p) and (g, h) == (3, 0) and not is_last(p - 1):
                            glu_a(p - 1, 1)
                    if scores_here(p):
                        split_m(p, g, 0)
                    if norm_here(p, g) and g == 0 and not scores_here(p):
                        normalise(p, g, 3)
                    here = prev2_here(p) and g == 0 and not is_last(p - 2)
                    if here:
                        glu_a(p - 2, 6)
                    if prev_here(p) and g == 1:
                        residual_sum(p - 1, 1 - par)
                    if prev_here(p) and g == 2:
                        best(p - 1, 1)
                    if scores_here(p):
                        split_m(p, g, 1)
                    if prev_here(p) and g == 2:
                        best(p - 1, 2)
                    if prev_here(p) and g == 1:
                        norm_x1(p - 1, 1 - par, 0)
                    if prev2_here(p) and g == 2 and p.known and p.v >= PAIRS:
                        add_y(p - 2, par)
                    if prev_here(p) and g == 3 and not is_last(p - 1):
                        glu_a(p - 1, 3)
                    if here:
                        glu_b(p - 2, 6)
                        glu_a(p - 2, 7)
                    if norm_here(p, g) and g == 2:
                        normalise(p, g, 3)
                    if scores_here(p):
                        add_m(p, g)
                    if prev_here(p) and g == 2:
                        for e in range(UGS if is_last(p - 1) else 1):
                            glu_a(p - 1, e)
                    if here:
                        glu_b(p - 2, 7)
                    if norm_here(p, g) and g == 0 and scores_here(p):
                        normalise(p, g, 3)
                    if prev_here(p) and g == 1:
                        norm_x1(p - 1, 1 - par, 1)
                    if prev_here(p) and g == 3 and not is_last(p - 1):
                        glu_b(p - 1, 3)

            nc.vector.memset(mpl[:], 0.0)
            for k in range(2):
                norm_x(Pair(0), 0, k)
            nc.vector.memset(kM[:, 0:2].bitcast(F32), 0.0).then_inc(zeroed, 1)
            dve.wait_ge(tables_in, 16)
            nc.vector.tensor_copy(ident_b[:], ident).then_inc(consts_r, 1)
            rotate(Pair(0), 1)
            rotate(Pair(0), 0)
            nc.vector.tensor_tensor(rot_a[:, 0, :], qk[:, 0, :], cosT, ALU.mult).then_inc(q_split, 1)
            dve.wait_ge(q_rotated, 1)
            nc.vector.tensor_tensor(rot_b[:, 0, :], rotated[:, 0, :], sinT, ALU.mult).then_inc(q_split, 1)
            dve.wait_ge(q_split, 2)
            nc.vector.tensor_tensor(roped[:, 0, :], rot_a[:, 0, :], rot_b[:, 0, :], ALU.add).then_inc(q_split, 1)
            dve.wait_ge(q_split, 3)
            nc.vector.tensor_copy(qk_hi[:, 0, 0, :], roped[:, 0, :]).then_inc(q_split, 1)
            dve.wait_ge(q_split, 4)
            nc.vector.tensor_tensor(qk_lo[:, 0, 0, :], roped[:, 0, :], qk_hi[:, 0, 0, :].bitcast(F32),
                                    ALU.subtract).then_inc(q_split, 1)
            dve.wait_ge(x_normed, 1)
            for k in range(2):
                norm_x(Pair(1), 1, k)
            dve.wait_ge(tanh_g, 1)
            dve.wait_ge(bv_projected, 1)
            nc.vector.tensor_scalar(tgo[:], up_bank[0][:, 0:1], vec[:, 2:3], tg[:, 0:1], ALU.add, ALU.mult)
            nc.vector.tensor_scalar(tgh[:], tg[:, 1:2], 0.5, None, ALU.mult).then_inc(gates_ready, 1)
            bodies(dve, body)

        @block.gpsimd
        def _(pool):
            def rope(p, n, k):
                s = q_split if n == 0 else k_split
                if k == 0:
                    pool.wait_ge(q_copied if n == 0 else k_copied, p.times(1, 1))
                    nc.gpsimd.tensor_tensor(rot_a[:, n, :], qk[:, n, :], cosT, ALU.mult).then_inc(s, 1)
                else:
                    pool.wait_ge(q_rotated if n == 0 else k_rotated, p.times(1, 1))
                    nc.gpsimd.tensor_tensor(rot_b[:, n, :], rotated[:, n, :], sinT, ALU.mult).then_inc(s, 1)

            def split_qk(p, par, n, k):
                s = q_split if n == 0 else k_split
                if k == 0:
                    pool.wait_ge(s, p.times(ROPES, 2))
                    nc.gpsimd.tensor_tensor(roped[:, n, :], rot_a[:, n, :], rot_b[:, n, :], ALU.add).then_inc(s, 1)
                elif k == 1:
                    pool.wait_ge(s, p.times(ROPES, 3))
                    if p.after(4, -4):
                        pool.wait_ge(stacked, p.times(4, -4))
                    settled(pool)
                    nc.gpsimd.tensor_copy(qk_hi[:, par, n, :], roped[:, n, :]).then_inc(s, 1)
                else:
                    pool.wait_ge(s, p.times(ROPES, 4))
                    nc.gpsimd.tensor_tensor(qk_lo[:, par, n, :], roped[:, n, :], qk_hi[:, par, n, :].bitcast(F32),
                                            ALU.subtract).then_inc(s, 1)

            def split_h(p, r):
                pool.wait_ge(h_copied, p.times(3, r + 1))
                chunks = slice(4 * r, min(4 * r + 4, FCH))
                nc.gpsimd.tensor_tensor(hT_lo[:, chunks, :], hT[:, chunks, :], hT_hi[:, chunks, :].bitcast(F32),
                                        ALU.subtract).then_inc(h_split, 1)

            def split_w(n):
                pool.wait_ge(w_rounded, n + 1)
                nc.gpsimd.tensor_tensor(piece((wup_lo[:], wdn_lo[:]), n), staged(n),
                                        piece((wup_hi[:].bitcast(F32), wdn_hi[:].bitcast(F32)), n),
                                        ALU.subtract).then_inc(w_split, 1)

            def residual(p, par):
                pool.wait_ge(x_in[par], p.times(16, 32 - 16 * par))
                if p.after(1, -1):
                    pool.wait_ge(x1_done, p.times(1, -1))
                settled(pool)
                nc.gpsimd.tensor_scalar(xres[:, par, :], xt[:, par, :], tgo[:, 0:1], None,
                                        ALU.add).then_inc(xres_done, 1)

            def inverse_root(p, s, steps, done, per, agg, shifted, inv):
                pool.wait_ge(s, p.times(steps, 2))
                settled(pool)
                nc.gpsimd.tensor_scalar(shifted[:], agg[:, 1:2], EPS, None, ALU.add).then_inc(done, 1)
                pool.wait_ge(done, p.times(per, 1))
                nc.gpsimd.tensor_tensor(inv[:], shifted[:], powers[:, 0:1], ALU.pow).then_inc(done, 1)

            def root_x(p):
                if p.after(1, 0):
                    pool.wait_ge(x_normed, p.times(1, 0))
                inverse_root(p, ln1, 2, root1, 3, mv, veps, rstd)
                pool.wait_ge(root1, p.times(3, 2))
                settled(pool)
                nc.gpsimd.tensor_scalar(shift[:], mv[:, 0:1], rstd[:, 0:1], -1.0, ALU.mult, ALU.mult).then_inc(root1, 1)

            def root_x1(p):
                inverse_root(p, ln2, 3, root2, 2, mv2, veps2, rstd2)

            def route(p):
                pool.wait_ge(dexp_done, p.times(1, 1))
                if p.after(2, 0):
                    pool.wait_ge(weighted, p.times(2, 0))
                settled(pool)
                nc.gpsimd.tensor_scalar(rt[:, 1:2], rt[:, 0:1], 1.0, None, ALU.add).then_inc(routed, 1)
                pool.wait_ge(routed, p.times(ROUTES, 1))
                nc.gpsimd.tensor_tensor(rt[:, 2:3], rt[:, 1:2], powers[:, 1:2], ALU.pow).then_inc(routed, 1)
                pool.wait_ge(top2, p.times(3, 3))
                settled(pool)
                nc.gpsimd.tensor_scalar(oh[:, 1, :], iota8, idxf[:, 1:2], rt[:, 0:1], ALU.is_equal,
                                        ALU.mult).then_inc(routed, 1)

            def body(p, par):
                halves = prev2_here(p) and not is_last(p - 2)
                if next_here(p):
                    rope(p + 1, 0, 0)
                if halves:
                    split_h(p - 2, 0)
                    split_h(p - 2, 1)
                if next_here(p):
                    rope(p + 1, 0, 1)
                    split_qk(p + 1, 1 - par, 0, 0)
                    split_qk(p + 1, 1 - par, 0, 1)
                if halves:
                    split_h(p - 2, 2)
                if next_here(p):
                    split_qk(p + 1, 1 - par, 0, 2)
                if p.known and p.v == 0:
                    split_w(0)
                if prev_here(p):
                    root_x1(p - 1)
                if next_here(p):
                    rope(p + 1, 1, 0)
                    rope(p + 1, 1, 1)
                if next_here(p):
                    for k in range(3):
                        split_qk(p + 1, 1 - par, 1, k)
                if p.known and p.v == 0:
                    split_w(1)
                if prev_here(p):
                    route(p - 1)
                if next2_here(p):
                    root_x(p + 2)
                if next_here(p):
                    residual(p + 1, 1 - par)
                if p.known and p.v < 2:
                    split_w(2 + 2 * p.v)
                    split_w(3 + 2 * p.v)

            nc.gpsimd.memset(powers[:, 0:1], -0.5)
            nc.gpsimd.memset(powers[:, 1:2], -1.0).then_inc(pool_consts, 1)
            nc.gpsimd.memset(sel_r[:].bitcast(F32), 0.0).then_inc(sel_zeroed, 1)
            nc.gpsimd.memset(vE[:], 1.0).then_inc(pool_consts, 1)
            pool.wait_ge(pool_consts, 1)
            root_x(Pair(0))
            pool.wait_ge(tables_in, 16)
            rope(Pair(0), 1, 0)
            rope(Pair(0), 1, 1)
            for k in range(3):
                split_qk(Pair(0), 0, 1, k)
            nc.gpsimd.memset(kM[:, 2:4].bitcast(F32), 0.0).then_inc(zeroed, 1)
            root_x(Pair(1))
            pool.wait_ge(gates_ready, 1)
            residual(Pair(0), 0)
            bodies(pool, body)


_OUTS = [((B, C, T), "float32")]


def kernel(**inputs):
    import numpy as _np
    import concourse.bacc as _bacc
    from concourse import mybir as _mybir
    from concourse.bass_utils import run_bass_kernel_spmd as _run

    a = {k: _np.asarray(v) for k, v in inputs.items()}
    wq, wk, wv = (a["L0_xattn_W" + n] for n in "qkv")
    bq, bk, bo = (a["L0_xattn_b" + n] for n in "qko")
    w_proj = _np.zeros((2, C, 3, 2, C), wq.dtype)
    for b in range(2):
        for n, w in enumerate((wq, wk, wv)):
            w_proj[b, :, n, b, :] = w.T
    w_proj = w_proj.reshape(P, 3, P)
    vecs = _np.stack([_np.concatenate([v, v]) for v in (bq, bk, bo)], axis=1)
    w_o = _np.zeros((2, GH, 32, C + 1), a["L0_xattn_Wo"].dtype)
    w_o[:, :, :KCH, :C] = a["L0_xattn_Wo"].T.reshape(2, GH, KCH, C)
    w_o[:, :, :KCH, C] = a["L0_xattn_bv"].reshape(2, GH, KCH)
    w_o = w_o.reshape(2, P, C + 1).transpose(1, 0, 2)
    gates = _np.concatenate([a["g_xattn"], a["g_ffn"]])[None, :]
    up = _np.concatenate([a["L0_ffn_W1"], a["L0_ffn_W2"]], axis=1).reshape(E * UP, T)
    w_up = _np.concatenate([a["L0_ffn_Wg"], up], axis=0).T
    w_down = a["L0_ffn_W3"].transpose(0, 2, 1).reshape(FCH, P, T).transpose(1, 0, 2)
    given = {"x": a["x"], "ctx": a["ctx_2048"], "w_proj": w_proj, "w_o": w_o, "vecs": vecs,
             "gates": gates, "w_up": w_up, "w_down": w_down, "const": constants()}

    nc = _bacc.Bacc("TRN2", target_bir_lowering=False, num_devices=1)
    arrays, args = {}, []
    for name, v in given.items():
        v = _np.ascontiguousarray(v)
        arrays[f"in_{name}_dram"] = v
        args.append(nc.dram_tensor(f"in_{name}_dram", v.shape, _mybir.dt.from_np(v.dtype), kind="ExternalInput").ap())
    for i, (shape, dtype) in enumerate(_OUTS):
        dt = _mybir.dt.from_np(_np.dtype(dtype))
        args.append(nc.dram_tensor(f"out_{i}_dram", shape, dt, kind="ExternalOutput").ap())
    build(nc, *args)
    r = _run(nc, [arrays], core_ids=[0])
    return r.results[0]["out_0_dram"]
```
